# Optimizing a Trainium2 kernel written in Bass

```python
import numpy as np
import jax
import jax.numpy as jnp

def _softmax(x, axis=-1):
    return jax.nn.softmax(x, axis=axis)

def _gelu(x):
    return jax.nn.gelu(x, approximate=True)

def _silu(x):
    return jax.nn.silu(x)

def _sigmoid(x):
    return jax.nn.sigmoid(x)

def _layernorm(x, axis=-1, eps=1e-05):
    m = jnp.mean(x, axis=axis, keepdims=True)
    v = jnp.var(x, axis=axis, keepdims=True)
    return (x - m) / jnp.sqrt(v + eps)

def _scatter_add(tgt, idx, src, axis=0):
    return tgt.at[idx].add(src)

def _segment_sum(src, seg, n):
    return jax.ops.segment_sum(src, seg, n)
kernel_name = 'mk_lm_tower_d1_tok_ids1024_r4_374486'

def setup_inputs(seed: int=0):
    np.random.seed(seed)
    _w = jnp.asarray

    def _rec_inputs():
        import jax
        import jax.numpy as jnp
        _rk = jax.random.key(seed)
        x = jax.random.randint(jax.random.fold_in(_rk, 1), (16, 512), 0, 12564, jnp.int32)
        return x
    x = _rec_inputs()

    def _L0_tok_setup():
        import jax, jax.numpy as jnp
        import numpy as np
        TOKENS = 50257
        DIMS = 256
        BATCH = 4
        SEQ = 1024
        key = jax.random.key(seed)
        k1, k2 = jax.random.split(key)
        x = jax.random.randint(k1, (BATCH, SEQ), 0, TOKENS, dtype=jnp.int64 if jax.config.jax_enable_x64 else jnp.int32)
        W = jax.random.normal(k2, (DIMS, TOKENS), dtype=jnp.float32) * (1.0 / np.sqrt(TOKENS))
        return {'x': x, 'W': W}
    _L0_tok_all = _L0_tok_setup()
    _L0_tok_in = {k: v for k, v in _L0_tok_all.items() if k in ('W',)}
    del _L0_tok_all

    def _L0_attn_setup():
        import jax, jax.numpy as jnp
        import numpy as np
        B_SZ, T, D_IN, H = (8, 256, 256, 256)
        key = jax.random.key(seed)
        ks = jax.random.split(key, 9)
        lim_u = 1.0 / np.sqrt(D_IN)
        return {'x': jax.random.normal(ks[0], (B_SZ, T, D_IN), dtype=jnp.float32), 'W_u': jax.random.uniform(ks[1], (H, D_IN), jnp.float32, -lim_u, lim_u), 'b_u': jax.random.uniform(ks[2], (H,), jnp.float32, -lim_u, lim_u), 'W_g': jax.random.uniform(ks[3], (H, D_IN), jnp.float32, -lim_u, lim_u), 'b_g': jax.random.uniform(ks[4], (H,), jnp.float32, -lim_u, lim_u), 'A': jnp.eye(H, dtype=jnp.float32) * 0.6, 'Bm': jax.random.normal(ks[5], (H, H), dtype=jnp.float32), 'Cm': jax.random.normal(ks[6], (H, H), dtype=jnp.float32), 'D': jax.random.normal(ks[7], (H,), dtype=jnp.float32)}
    _L0_attn_all = _L0_attn_setup()
    _L0_attn_in = {k: v for k, v in _L0_attn_all.items() if k in ('W_u', 'b_u', 'W_g', 'b_g', 'A', 'Bm', 'Cm', 'D')}
    del _L0_attn_all

    def _L0_ffn_setup():
        import jax, jax.numpy as jnp
        import numpy as np
        DIM = 256
        HIDDEN = 768
        SCALE = 1.0 / 127.0

        def _dequant(w_int, dtype):
            return w_int.astype(dtype) * jnp.asarray(SCALE, dtype)
        key = jax.random.key(seed)
        k_x, k_g, k_u, k_d = jax.random.split(key, 4)
        x = jax.random.normal(k_x, (4, 512, DIM), dtype=jnp.float32)
        w_gate = jax.random.randint(k_g, (HIDDEN, DIM), -127, 128, dtype=jnp.int32)
        w_up = jax.random.randint(k_u, (HIDDEN, DIM), -127, 128, dtype=jnp.int32)
        w_down = jax.random.randint(k_d, (DIM, HIDDEN), -127, 128, dtype=jnp.int32)
        return {'x': x, 'w_gate': w_gate, 'w_up': w_up, 'w_down': w_down}
    _L0_ffn_all = _L0_ffn_setup()
    _L0_ffn_in = {k: v for k, v in _L0_ffn_all.items() if k in ('w_gate', 'w_up', 'w_down')}
    del _L0_ffn_all
    return {'x': x, 'L0_tok_W': _L0_tok_in['W'], 'L0_attn_W_u': _L0_attn_in['W_u'], 'L0_attn_b_u': _L0_attn_in['b_u'], 'L0_attn_W_g': _L0_attn_in['W_g'], 'L0_attn_b_g': _L0_attn_in['b_g'], 'L0_attn_A': _L0_attn_in['A'], 'L0_attn_Bm': _L0_attn_in['Bm'], 'L0_attn_Cm': _L0_attn_in['Cm'], 'L0_attn_D': _L0_attn_in['D'], 'L0_ffn_w_gate': _L0_ffn_in['w_gate'], 'L0_ffn_w_up': _L0_ffn_in['w_up'], 'L0_ffn_w_down': _L0_ffn_in['w_down']}

def reference(x, L0_tok_W, L0_attn_W_u, L0_attn_b_u, L0_attn_W_g, L0_attn_b_g, L0_attn_A, L0_attn_Bm, L0_attn_Cm, L0_attn_D, L0_ffn_w_gate, L0_ffn_w_up, L0_ffn_w_down):
    import jax
    import jax.numpy as jnp

    def _L0_tok_ref(x, W):
        import jax, jax.numpy as jnp
        import numpy as np
        TOKENS = 50257
        DIMS = 256
        BATCH = 4
        SEQ = 1024
        return jnp.take(W.T, x, axis=0)

    def _L0_attn_ref(x, W_u, b_u, W_g, b_g, A, Bm, Cm, D):
        import jax, jax.numpy as jnp
        import numpy as np
        B_SZ, T, D_IN, H = (8, 256, 256, 256)
        u = jax.nn.gelu(jnp.einsum('btd,hd->bth', x, W_u) + b_u, approximate=False) * jax.nn.sigmoid(jnp.einsum('btd,hd->bth', x, W_g) + b_g)
        uB = jnp.einsum('btd,hd->tbh', u, Bm)

        def step(s, uB_t):
            s = s @ A.T + uB_t
            y = s @ Cm.T + D
            return (s, y)
        s0 = jnp.zeros((x.shape[0], A.shape[0]), dtype=x.dtype)
        _, ys = jax.lax.scan(step, s0, uB)
        return jnp.transpose(ys, (1, 0, 2))

    def _L0_ffn_ref(x, w_gate, w_up, w_down):
        import jax, jax.numpy as jnp
        import numpy as np
        DIM = 256
        HIDDEN = 768
        SCALE = 1.0 / 127.0

        def _dequant(w_int, dtype):
            return w_int.astype(dtype) * jnp.asarray(SCALE, dtype)
        wg = _dequant(w_gate, x.dtype)
        wu = _dequant(w_up, x.dtype)
        wd = _dequant(w_down, x.dtype)
        gate = jnp.einsum('bsd,hd->bsh', x, wg)
        up = jnp.einsum('bsd,hd->bsh', x, wu)
        h = jax.nn.silu(gate) * up
        return jnp.einsum('bsh,dh->bsd', h, wd)
    h = _L0_tok_ref(x, L0_tok_W)
    h = h + _L0_attn_ref(_layernorm(h, axis=-1), L0_attn_W_u, L0_attn_b_u, L0_attn_W_g, L0_attn_b_g, L0_attn_A, L0_attn_Bm, L0_attn_Cm, L0_attn_D)
    h = h + _L0_ffn_ref(_layernorm(h, axis=-1), L0_ffn_w_gate, L0_ffn_w_up, L0_ffn_w_down)
    return h

_drawn_inputs = setup_inputs


def setup_inputs(seed=0):
    import zlib

    import numpy as np

    out = dict(_drawn_inputs(seed))
    spreads = {}
    factors = {}
    for name, (base, spread) in spreads.items():
        noise = np.random.default_rng([zlib.crc32(name.encode()), seed]).standard_normal(out[name].shape)
        drawn = base * np.exp(spread * noise) if base else spread * noise
        out[name] = jnp.asarray(drawn.astype(out[name].dtype))
    for name, factor in factors.items():
        out[name] = (out[name] * factor).astype(out[name].dtype)
    return out
```

```python
from contextlib import ExitStack

import concourse.bass as bass
from concourse import mybir

F32 = mybir.dt.float32
F32R = mybir.dt.float32r
I32 = mybir.dt.int32
ALU = mybir.AluOpType
ACT = mybir.ActivationFunctionType

P = 128
BATCH, SEQ, DIM = 16, 512, 256
STEPS = 16
CHUNKS = SEQ // STEPS
COLS = BATCH * CHUNKS
GROUPS = COLS // P
KD = DIM // P
HIDDEN = 768
KH = HIDDEN // P
HI, LO = 0, 1
SCALE = 1.0 / 127.0
EPS = 1e-5
SPLIT = ((HI, HI), (HI, LO), (LO, HI))
H_SLOTS = 3


def build(nc, x, table, wu, bu, wg, bg, a_t, a_n, bm, cm, d, w_gate, w_up, w_down, out):
    ctx = ExitStack()
    phase1 = ExitStack()
    phase2 = ExitStack()
    with ctx:
        def sb(name, shape, dt, stack=ctx):
            return stack.enter_context(nc.sbuf_tensor(name, shape, dt))

        def sem(name):
            return ctx.enter_context(nc.semaphore(name))

        hres = sb("hres", [P, STEPS * GROUPS, DIM], F32)
        w_gu = sb("w_gu", [P, 2, KD, 2 * HIDDEN], F32R)
        w_dn = sb("w_dn", [P, 2, KH, DIM], F32R)
        xn = sb("xn", [P, GROUPS, DIM], F32)
        xT = sb("xT", [P, 2, KD, COLS], F32R)
        sT = sb("sT", [P, 2, KD, COLS], F32R)
        split12 = sb("split12", [P, 12 * DIM], F32R)
        work8 = sb("work8", [P, 4, COLS], F32)
        ident = sb("ident", [P, P], F32)
        bias = sb("bias", [P, 2, KD], F32)
        bn = sb("bn", [P, GROUPS, 6], F32)
        mv = sb("mv", [P, GROUPS, 2], F32)
        var_eps = sb("var_eps", [P, GROUPS], F32)
        rstd = sb("rstd", [P, GROUPS], F32)
        neg_half = sb("neg_half", [P, GROUPS], F32)
        lo_max = sb("lo_max", [P, 2], F32)
        lo_all = sb("lo_all", [P, 1], F32)
        wide = sb("wide", [P, 1], I32)
        m16 = sb("m16", [P, KD, DIM], F32)

        an = split12[:, 0:4 * DIM].rearrange("p (s k n) -> p s k n", s=2, k=KD)
        ct = split12[:, 4 * DIM:8 * DIM].rearrange("p (s k n) -> p s k n", s=2, k=KD)
        hT = split12[:, :].rearrange("p (m s n) -> p m s n", m=H_SLOTS, s=2)
        s_end = work8[:, 0:2, :]
        start = work8[:, 2:4, :].rearrange("p k (b c) -> p k b c", c=CHUNKS)
        silu = work8[:, 0:2, :]
        hid = work8[:, 2:4, :]

        raw = sb("raw", [P, 6, KD, DIM], F32, phase1)
        w1 = sb("w1", [P, 4, 2, KD, DIM], F32R, phase1)
        stage = sb("stage", [P, 2, GROUPS, DIM], F32, phase1)
        idx_t = sb("idx_t", [P, 2, GROUPS], I32, phase1)
        idx = sb("idx", [P, GROUPS, STEPS], I32, phase1)
        d_row = sb("d_row", [P, DIM], F32, phase1)
        acts = sb("acts", [P, 4, COLS], F32, phase1)
        v = sb("v", [P, KD, COLS], F32, phase1)
        vT = sb("vT", [P, 2, KD, COLS], F32R, phase1)
        raw_gu = sb("raw_gu", [P, KD, HIDDEN], I32, phase1)
        gelu, tanh = acts[:, 0:2, :], acts[:, 2:4, :]
        pw = acts[:, :, :].rearrange("p (b s) (k n) -> p b s k n", b=2, k=KD)
        raw_dn = raw[:, 0:3, :, :].rearrange("p a k n -> p (a k) n").bitcast(I32)
        at, wut, wgt, bt = 0, 1, 2, 3
        phase1.close()
        hm = sb("hm", [P, STEPS, 2, KD, DIM], F32R, phase2)
        phase2.close()

        xt_ps = ctx.enter_context(nc.psum_tensor("xt_ps", [P, 2, COLS], F32))
        up_ps = ctx.enter_context(nc.psum_tensor("up_ps", [P, 4, COLS], F32))
        st_ps = ctx.enter_context(nc.psum_tensor("st_ps", [P, 2, COLS], F32))
        tok_ps = xt_ps[:, :, :].rearrange("p b (g n) -> p b g n", n=DIM)
        dn_ps = st_ps[:, :, :].rearrange("p b (g n) -> p b g n", n=DIM)

        ld_idx, ld_a, ld_w, ld_small, ld_gu, ld_dn = (sem(n) for n in
                                                      ("ld_idx", "ld_a", "ld_w", "ld_small", "ld_gu", "ld_dn"))
        gathered = [sem("gathered0"), sem("gathered1")]
        idx_set = sem("idx_set")
        const_set = sem("const_set")
        ident_set = sem("ident_set")
        hres_set = sem("hres_set")
        bn_set = sem("bn_set")
        mv_set = sem("mv_set")
        eps_set = sem("eps_set")
        rstd_set = sem("rstd_set")
        xn_set = sem("xn_set")
        xt_done = sem("xt_done")
        xhi_set = sem("xhi_set")
        xlo_set = sem("xlo_set")
        whi_set = sem("whi_set")
        wlo_set = sem("wlo_set")
        ffhi_set = sem("ffhi_set")
        fflo_set = sem("fflo_set")
        lomax_set = sem("lomax_set")
        loall_set = sem("loall_set")
        wide_set = sem("wide_set")
        bias_set = sem("bias_set")
        pow_done = sem("pow_done")
        pow_set = sem("pow_set")
        ug_done = sem("ug_done")
        act_set = sem("act_set")
        v_set = sem("v_set")
        vhi_set = sem("vhi_set")
        vlo_set = sem("vlo_set")
        bv_done = sem("bv_done")
        s_done = sem("s_done")
        shi_set = sem("shi_set")
        slo_set = sem("slo_set")
        y_done = sem("y_done")
        y_added = sem("y_added")
        send_set = sem("send_set")
        zero_set = sem("zero_set")
        start_set = sem("start_set")
        bst_done = sem("bst_done")
        hm_done = sem("hm_done")
        hmhi_set = sem("hmhi_set")
        hmlo_set = sem("hmlo_set")
        starthi_set = sem("starthi_set")
        startlo_set = sem("startlo_set")
        corr_done = sem("corr_done")
        h2_set = sem("h2_set")
        gu_done = sem("gu_done")
        silu_set = sem("silu_set")
        hid_set = sem("hid_set")
        hhi_set = sem("hhi_set")
        hlo_set = sem("hlo_set")
        dn_done = sem("dn_done")
        out_set = sem("out_set")
        stored = sem("stored")

        block = ctx.enter_context(nc.Block())
        out_v = out.rearrange("(g p j) d -> p g j d", p=P, j=STEPS)

        def inside(t, first, end):
            return first <= t < end if isinstance(t, int) else True

        carrier = {e.engine: e.alloc_register("wait_carrier") for e in (nc.vector, nc.gpsimd)}

        def wait_alone(eng, semaphore, count):
            if not isinstance(count, int):
                eng.reg_add(carrier[eng.engine], count, 0)
                count = carrier[eng.engine]
            eng.wait_ge(const_set, 2)
            eng.wait_ge(semaphore, count)

        def tiles(t):
            return hres[:, bass.ds(t * GROUPS, GROUPS), :]

        @block.sync
        def _(sp):
            sp.dma_start(idx[:, :, :], x.rearrange("(g p j) -> p g j", p=P, j=STEPS)).then_inc(ld_idx, 16)
            for n, w in enumerate((a_t, a_n)):
                sp.dma_start(raw[:, n, :, :], w.rearrange("(k p) n -> p k n", p=P)).then_inc(ld_a, 16)
            sp.dma_start(d_row[:, :], d.partition_broadcast(P)).then_inc(ld_small, 16)
            with nc.allow_non_contiguous_dma("two vectors of 256 values"):
                sp.dma_start(bias[:, 0, :], bu.rearrange("(k p) -> p k", p=P)).then_inc(ld_small, 16)
                sp.dma_start(bias[:, 1, :], bg.rearrange("(k p) -> p k", p=P)).then_inc(ld_small, 16)
            for n, w in enumerate((wu, wg, bm, cm)):
                sp.dma_start(raw[:, 2 + n, :, :], w.rearrange("(k p) n -> p k n", p=P)).then_inc(ld_w, 16)
            sp.dma_start(raw_gu[:, :, :], w_gate.rearrange("(k p) n -> p k n", p=P)).then_inc(ld_gu, 16)
            sp.wait_ge(whi_set, 6)
            sp.wait_ge(wlo_set, 6)
            sp.wait_ge(pow_done, 2)
            sp.dma_start(raw_dn, w_down.rearrange("(k p) n -> p k n", p=P)).then_inc(ld_dn, 16)
            sp.wait_ge(fflo_set, 1)
            sp.dma_start(raw_gu[:, :, :], w_up.rearrange("(k p) n -> p k n", p=P)).then_inc(ld_gu, 16)
            with sp.Fori(0, STEPS) as j:
                sp.wait_ge(out_set, 2 * j + 2)
                sp.dma_start(out_v[:, :, j, :], tiles(j)).then_inc(stored, 16)
            sp.wait_ge(stored, 16 * STEPS)

        @block.gpsimd
        def _(pool):
            pool.memset(ident[:, :], 0.0).then_inc(const_set, 1)
            pool.memset(neg_half[:, :], -0.5).then_inc(const_set, 1)
            pool.wait_ge(ld_idx, 16)

            def gather(j, p):
                pool.tensor_copy(idx_t[:, p, :], idx[:, :, j]).then_inc(idx_set, 1)
                wait_alone(pool, idx_set, j + 1)
                for g in range(GROUPS):
                    pool.indirect_dma_start(
                        out=stage[:, p, g, :], out_offset=None, in_=table,
                        in_offset=bass.IndirectOffsetOnAxis(ap=idx_t[:, p, g:g + 1], axis=0),
                    ).then_inc(gathered[p], 16)

            def rstd_of(n):
                wait_alone(pool, mv_set, n + 1)
                pool.tensor_scalar(var_eps[:, :], mv[:, :, 1], EPS, None, ALU.add).then_inc(eps_set, 1)
                pool.wait_ge(eps_set, n + 1)
                pool.tensor_tensor(rstd[:, :], var_eps[:, :], neg_half[:, :], ALU.pow).then_inc(rstd_set, 1)

            gather(0, 0)
            gather(1, 1)
            pool.wait_ge(const_set, 2)
            pool.affine_select(out=ident[:, :], in_=ident[:, :], compare_op=ALU.not_equal, fill=1.0, base=0,
                               pattern=[[-1, P]], channel_multiplier=1).then_inc(ident_set, 1)
            pool.wait_ge(ld_small, 48)

            def tile_in(j, p, n_even, more):
                pool.wait_ge(gathered[p], (n_even + 1) * GROUPS * 16)
                pool.tensor_tensor(tiles(j), stage[:, p, :, :],
                                   d_row[:, None, :].to_broadcast([P, GROUPS, DIM]), ALU.add).then_inc(hres_set, 1)
                rstd_of(j)
                if more:
                    pool.wait_ge(xn_set, j + 1)
                    pool.wait_ge(hres_set, j + 1)
                    gather(j + 2, p)

            with pool.Fori(0, STEPS // 2 - 1) as i:
                tile_in(2 * i, 0, i, True)
                tile_in(2 * i + 1, 1, i, True)
            tile_in(STEPS - 2, 0, STEPS // 2 - 1, False)
            tile_in(STEPS - 1, 1, STEPS // 2 - 1, False)

            pool.wait_ge(ld_gu, 16)
            pool.tensor_copy(w_gu[:, HI, :, 0:HIDDEN], raw_gu[:, :, :]).then_inc(ffhi_set, 1)
            pool.wait_ge(ld_dn, 16)
            pool.tensor_copy(w_dn[:, HI, :, :], raw_dn).then_inc(ffhi_set, 1)
            pool.wait_ge(ld_gu, 32)
            pool.tensor_copy(w_gu[:, HI, :, HIDDEN:], raw_gu[:, :, :]).then_inc(ffhi_set, 1)
            pool.wait_ge(lomax_set, 3)
            pool.partition_all_reduce(lo_all[:, :], lo_max[:, 0:1], P, bass.bass_isa.ReduceOp.max).then_inc(loall_set, 1)

            def hid_lo(j, m):
                pool.wait_ge(hhi_set, KH * j + m + 1)
                pool.tensor_tensor(hT[:, m % H_SLOTS, LO, :], hid[:, m % 2, :],
                                   hT[:, m % H_SLOTS, HI, :].bitcast(F32), ALU.subtract).then_inc(hlo_set, 1)

            rstd_of(STEPS)

            def tile_ff(j, more):
                for m in range(KH):
                    hid_lo(j, m)
                    if m == 2 and more:
                        rstd_of(STEPS + j + 1)

            with pool.Fori(0, STEPS - 1) as j:
                tile_ff(j, True)
            tile_ff(STEPS - 1, False)

        @block.tensor
        def _(pe):
            def product(ps, w, m, r, first=True, last=True):
                n = 0
                for k in range(KD):
                    for ws, rs in SPLIT:
                        mm = pe.matmul(ps, w[:, ws, k, m * P:(m + 1) * P], r[:, rs, k, :],
                                       start=first and n == 0, stop=last and n == KD * len(SPLIT) - 1)
                        n += 1
                return mm

            def transposes(n):
                pe.wait_ge(xn_set, n + 1)
                for k in range(KD):
                    for g in range(GROUPS):
                        t = pe.transpose(xt_ps[:, k, g * P:(g + 1) * P], xn[:, g, k * P:(k + 1) * P], ident[:, :])
                    t.then_inc(xt_done, 1)

            def tokens(w, r, done):
                for b in range(2):
                    for g in range(2):
                        n = 0
                        for k in range(KD):
                            for ws, rs in SPLIT:
                                c = (2 * b + g) * P
                                mm = pe.matmul(tok_ps[:, b, g, :], w[:, ws, k, c:c + P], r[:, rs, k, :],
                                               start=n == 0, stop=n == KD * len(SPLIT) - 1)
                                n += 1
                    mm.then_inc(done, 1)

            pe.wait_ge(ld_a, 32)
            for r in range(4):
                if r:
                    pe.wait_ge(pow_set, 2 * r)
                src_t = raw[:, 0, :, :] if r == 0 else pw[:, (r - 1) % 2, 0, :, :]
                src_n = raw[:, 1, :, :] if r == 0 else pw[:, (r - 1) % 2, 1, :, :]
                for side in range(2 if r < 3 else 1):
                    w, mv_ = (src_n, src_t) if side == 0 else (src_t, src_n)
                    for m in range(KD):
                        for k in range(KD):
                            mm = pe.matmul(up_ps[:, 2 * (r % 2) + side, m * DIM:(m + 1) * DIM],
                                           w[:, k, m * P:(m + 1) * P], mv_[:, k, :], start=k == 0, stop=k == KD - 1)
                    mm.then_inc(pow_done, 1)

            def ug(j, m):
                pe.wait_ge(xlo_set, 2 * j + 2)
                if inside(j, 1, STEPS):
                    pe.wait_ge(act_set, 2 * j + m - 1)
                product(up_ps[:, 2 * m, :], w1[:, wut], m, xT)
                product(up_ps[:, 2 * m + 1, :], w1[:, wgt], m, xT).then_inc(ug_done, 1)

            def states(j):
                pe.wait_ge(vlo_set, 2 * j + 2)
                if inside(j, 1, STEPS):
                    pe.wait_ge(slo_set, 2 * j)
                for m in range(KD):
                    mm = product(st_ps[:, m, :], w1[:, bt], m, vT, last=not inside(j, 1, STEPS))
                    if not inside(j, 1, STEPS):
                        mm.then_inc(s_done, 1)
                if not inside(j, 1, STEPS):
                    return
                mm.then_inc(bv_done, 1)
                for m in range(KD):
                    product(st_ps[:, m, :], w1[:, at], m, sT, first=False).then_inc(s_done, 1)

            def outputs(j):
                pe.wait_ge(slo_set, 2 * j + 2)
                pe.wait_ge(xlo_set, min(2 * (j + 3), 2 * STEPS) if isinstance(j, int) else 2 * (j + 3))
                if inside(j, 1, STEPS):
                    pe.wait_ge(y_added, 2 * j)
                tokens(sT, ct, y_done)

            def step(j):
                if inside(j, 0, STEPS - 1):
                    ug(j + 1, 0)
                if inside(j, 1, STEPS):
                    outputs(j - 1)
                if inside(j, 0, STEPS - 1):
                    ug(j + 1, 1)
                if inside(j, 0, STEPS - 2):
                    if inside(j, 1, STEPS):
                        pe.wait_ge(y_added, 2 * j)
                    else:
                        pe.wait_ge(xlo_set, 4)
                    transposes(j + 2)
                states(j)

            pe.wait_ge(ident_set, 1)
            transposes(0)
            pe.wait_ge(whi_set, 6)
            pe.wait_ge(wlo_set, 6)
            pe.wait_ge(pow_set, 7)
            ug(0, 0)
            ug(0, 1)
            transposes(1)
            step(0)
            with pe.Fori(1, STEPS - 2) as j:
                step(j)
            step(STEPS - 2)
            step(STEPS - 1)
            outputs(STEPS - 1)

            def hm_product(j, r):
                ps = up_ps[:, 0, :]
                for m in range(KD):
                    mm = product(ps[:, m * DIM:(m + 1) * DIM], an, m, r)
                mm.then_inc(hm_done, 1)

            def chunk(c):
                pe.wait_ge(start_set, c)
                for m in range(KD):
                    for k in range(KD):
                        mm = pe.matmul(up_ps[:, 2, m * BATCH:(m + 1) * BATCH], m16[:, k, m * P:(m + 1) * P],
                                       start[:, k, :, c], start=k == 0, stop=k == KD - 1)
                mm.then_inc(bst_done, 1)

            hm_product(0, ct)
            with pe.Fori(0, STEPS - 1) as r:
                chunk(2 * r + 1)
                pe.wait_ge(hmlo_set, r + 1)
                hm_product(r + 1, hm[:, r])
                chunk(2 * r + 2)

            def corrections(j):
                tokens(sT, hm[:, j], corr_done)

            def phase_2(lo_weights):
                parts = ((HI, HI), (HI, LO), (LO, HI)) if lo_weights else ((HI, HI), (HI, LO))

                def gate_up(j, m):
                    if m == 0:
                        pe.wait_ge(xlo_set, 2 * (j + STEPS) + 2)
                    if m >= 2 or inside(j, 1, STEPS):
                        pe.wait_ge(hid_set, KH * j + m - 1)
                    for side in range(2):
                        n = 0
                        for k in range(KD):
                            for ws, rs in parts:
                                c = side * HIDDEN + m * P
                                mm = pe.matmul(up_ps[:, 2 * (m % 2) + side, :], w_gu[:, ws, k, c:c + P],
                                               xT[:, rs, k, :], start=n == 0, stop=n == KD * len(parts) - 1)
                                n += 1
                    mm.then_inc(gu_done, 1)

                def down(j, m):
                    pe.wait_ge(hlo_set, KH * j + m + 1)
                    if m == 0 and inside(j, 1, STEPS):
                        pe.wait_ge(out_set, 2 * j)
                    for g in range(GROUPS):
                        for n, (ws, hs) in enumerate(parts):
                            mm = pe.matmul(dn_ps[:, g // 2, g % 2, :],
                                           hT[:, m % H_SLOTS, hs, g * P:(g + 1) * P], w_dn[:, ws, m, :],
                                           start=m == 0 and g % 2 == 0 and n == 0,
                                           stop=m == KH - 1 and n == len(parts) - 1, skip_group_check=True)
                    mm.then_inc(dn_done, 1)

                def step_2(j):
                    gate_up(j, 0)
                    if inside(j, 1, STEPS):
                        down(j - 1, KH - 1)
                    gate_up(j, 1)
                    if inside(j, 0, STEPS - 1):
                        corrections(j + 1)
                    gate_up(j, 2)
                    down(j, 0)
                    gate_up(j, 3)
                    down(j, 1)
                    gate_up(j, 4)
                    down(j, 2)
                    gate_up(j, 5)
                    if inside(j, 0, STEPS - 1):
                        transposes(STEPS + j + 1)
                    down(j, 3)
                    down(j, 4)

                step_2(0)
                with pe.Fori(1, STEPS - 1) as j:
                    step_2(j)
                step_2(STEPS - 1)
                down(STEPS - 1, KH - 1)

            pe.wait_ge(startlo_set, 2)
            pe.wait_ge(hmlo_set, STEPS)
            pe.wait_ge(y_added, 2 * STEPS)
            corrections(0)
            pe.wait_ge(h2_set, 2)
            transposes(STEPS)
            pe.wait_ge(wide_set, 1)
            pe.wait_ge(fflo_set, 3)
            is_wide = pe.value_load(wide[0:1, 0:1], min_val=0, max_val=1)
            with pe.If(is_wide == 0):
                phase_2(False)
            with pe.Else():
                phase_2(True)

        @block.scalar
        def _(act):
            def w_hi(dst, n):
                act.activation(dst[:, HI], raw[:, n, :, :], ACT.Copy).then_inc(whi_set, 1)

            act.wait_ge(ld_a, 32)
            w_hi(w1[:, at], 0)
            w_hi(an, 1)
            act.wait_ge(ld_w, 64)
            w_hi(w1[:, wut], 2)
            w_hi(w1[:, wgt], 3)
            w_hi(w1[:, bt], 4)
            w_hi(ct, 5)

            def x_hi(n):
                for k in range(KD):
                    act.wait_ge(xt_done, 2 * n + k + 1)
                    act.activation(xT[:, HI, k, :], xt_ps[:, k, :], ACT.Copy).then_inc(xhi_set, 1)

            def gates(j, m):
                act.wait_ge(ug_done, 2 * j + m + 1)
                if inside(j, 1, STEPS):
                    act.wait_ge(v_set, 2 * j + m - 1)
                act.activation(gelu[:, m, :], up_ps[:, 2 * m, :], ACT.Gelu, bias=bias[:, 0, m:m + 1])
                act.activation(tanh[:, m, :], up_ps[:, 2 * m + 1, :], ACT.Tanh, bias=bias[:, 1, m:m + 1],
                               scale=0.5).then_inc(act_set, 1)

            def v_hi(j):
                if inside(j, 1, STEPS):
                    if isinstance(j, int) and j == 1:
                        act.wait_ge(s_done, 2)
                    else:
                        act.wait_ge(bv_done, j - 1)
                for m in range(KD):
                    act.wait_ge(v_set, 2 * j + m + 1)
                    act.activation(vT[:, HI, m, :], v[:, m, :], ACT.Copy).then_inc(vhi_set, 1)

            def s_hi(j):
                act.wait_ge(s_done, 2 * j + 2)
                for m in range(KD):
                    act.activation(sT[:, HI, m, :], st_ps[:, m, :], ACT.Copy).then_inc(shi_set, 1)

            def step(j):
                if inside(j, 0, STEPS - 1):
                    gates(j + 1, 0)
                    gates(j + 1, 1)
                if inside(j, 0, STEPS - 2):
                    x_hi(j + 2)
                if inside(j, 0, STEPS - 1):
                    v_hi(j + 1)
                s_hi(j)

            x_hi(0)
            act.wait_ge(bias_set, 1)
            gates(0, 0)
            gates(0, 1)
            x_hi(1)
            v_hi(0)
            step(0)
            with act.Fori(1, STEPS - 2) as j:
                step(j)
            step(STEPS - 2)
            step(STEPS - 1)
            for m in range(KD):
                act.wait_ge(slo_set, 2 * STEPS - 1 + m)
                act.activation(s_end[:, m, :], st_ps[:, m, :], ACT.Copy).then_inc(send_set, 1)

            def hm_hi(j):
                act.wait_ge(hm_done, j + 1)
                act.activation(hm[:, j, HI, :, :], up_ps[:, 0, :], ACT.Copy).then_inc(hmhi_set, 1)

            with act.Fori(0, STEPS) as j:
                hm_hi(j)
            act.wait_ge(start_set, CHUNKS - 1)
            act.wait_ge(y_done, 2 * STEPS)
            act.wait_ge(zero_set, 1)
            for k in range(KD):
                act.activation(sT[:, HI, k, :], start[:, k, :, :], ACT.Copy).then_inc(starthi_set, 1)

            def silu_of(j, m):
                act.wait_ge(gu_done, KH * j + m + 1)
                if m >= 2 or inside(j, 1, STEPS):
                    act.wait_ge(hid_set, KH * j + m - 1)
                act.activation(silu[:, m % 2, :], up_ps[:, 2 * (m % 2), :], ACT.Silu,
                               scale=SCALE).then_inc(silu_set, 1)

            def hid_hi(j, m):
                act.wait_ge(hid_set, KH * j + m + 1)
                if m >= H_SLOTS or inside(j, 1, STEPS):
                    act.wait_ge(dn_done, KH * j + m + 1 - H_SLOTS)
                act.activation(hT[:, m % H_SLOTS, HI, :], hid[:, m % 2, :], ACT.Copy).then_inc(hhi_set, 1)

            def step_2(j):
                for m in range(KH):
                    silu_of(j, m)
                    if m:
                        hid_hi(j, m - 1)
                if inside(j, 0, STEPS - 1):
                    x_hi(STEPS + j + 1)
                hid_hi(j, KH - 1)

            x_hi(STEPS)
            step_2(0)
            with act.Fori(1, STEPS - 1) as j:
                step_2(j)
            step_2(STEPS - 1)

        @block.vector
        def _(dve):
            def w_lo(dst, n):
                dve.wait_ge(whi_set, n + 1)
                dve.tensor_tensor(dst[:, LO], raw[:, n, :, :], dst[:, HI].bitcast(F32),
                                  ALU.subtract).then_inc(wlo_set, 1)

            def norm_stats(n, src):
                if src is stage:
                    wait_alone(dve, hres_set, n + 1)
                for g in range(GROUPS):
                    rows = stage[:, n % 2, g, :] if src is stage else hres[:, (n - STEPS) * GROUPS + g, :]
                    last = dve.bn_stats(bn[:, g, :], rows)
                last.then_inc(bn_set, 1)
                wait_alone(dve, bn_set, n + 1)
                for g in range(GROUPS):
                    last = dve.bn_aggr(mv[:, g, :], bn[:, g, :])
                last.then_inc(mv_set, 1)

            def norm_apply(n, src):
                dve.wait_ge(rstd_set, n + 1)
                if not (isinstance(n, int) and n == 0):
                    dve.wait_ge(xt_done, 2 * n)
                for g in range(GROUPS):
                    rows = stage[:, n % 2, g, :] if src is stage else hres[:, (n - STEPS) * GROUPS + g, :]
                    last = dve.tensor_scalar(xn[:, g, :], rows, mv[:, g, 0:1], rstd[:, g:g + 1],
                                             ALU.subtract, ALU.mult)
                last.then_inc(xn_set, 1)

            def x_lo(n):
                for k in range(KD):
                    dve.wait_ge(xhi_set, 2 * n + k + 1)
                    dve.tensor_tensor(xT[:, LO, k, :], xt_ps[:, k, :], xT[:, HI, k, :].bitcast(F32),
                                      ALU.subtract).then_inc(xlo_set, 1)

            def gate(j, m):
                dve.wait_ge(act_set, 2 * j + m + 1)
                if inside(j, 1, STEPS):
                    dve.wait_ge(vlo_set, 2 * j + m - 1)
                dve.scalar_tensor_tensor(out=v[:, m, :], in0=tanh[:, m, :], scalar=1.0, in1=gelu[:, m, :],
                                         op0=ALU.add, op1=ALU.mult).then_inc(v_set, 1)

            def v_lo(j):
                for m in range(KD):
                    dve.wait_ge(vhi_set, 2 * j + m + 1)
                    dve.tensor_tensor(vT[:, LO, m, :], v[:, m, :], vT[:, HI, m, :].bitcast(F32),
                                      ALU.subtract).then_inc(vlo_set, 1)

            def s_lo(j):
                for m in range(KD):
                    dve.wait_ge(shi_set, 2 * j + m + 1)
                    dve.tensor_tensor(sT[:, LO, m, :], st_ps[:, m, :], sT[:, HI, m, :].bitcast(F32),
                                      ALU.subtract).then_inc(slo_set, 1)

            def add_tokens(j, done, added):
                for b in range(2):
                    dve.wait_ge(done, 2 * j + b + 1)
                    half = hres[:, bass.ds(j * GROUPS + 2 * b, 2), :]
                    dve.scalar_tensor_tensor(out=half, in0=tok_ps[:, b, :, :], scalar=0.5, in1=half,
                                             op0=ALU.mult, op1=ALU.add).then_inc(added, 1)

            def step(j):
                if inside(j, 0, STEPS - 1):
                    gate(j + 1, 0)
                if inside(j, 1, STEPS):
                    add_tokens(j - 1, y_done, y_added)
                if inside(j, 0, STEPS - 1):
                    gate(j + 1, 1)
                if inside(j, 0, STEPS - 3):
                    norm_stats(j + 3, stage)
                if inside(j, 0, STEPS - 2):
                    x_lo(j + 2)
                if inside(j, 0, STEPS - 1):
                    v_lo(j + 1)
                s_lo(j)
                if inside(j, 0, STEPS - 3):
                    norm_apply(j + 3, stage)

            def powers(r):
                for side in range(2 if r < 3 else 1):
                    dve.wait_ge(pow_done, 2 * r + side + 1)
                    dst = pw[:, r % 2, side, :, :] if r < 3 else m16[:, :, :]
                    dve.tensor_copy(dst, up_ps[:, 2 * (r % 2) + side, :].rearrange("p (k n) -> p k n", k=KD)
                                    ).then_inc(pow_set, 1)

            powers(0)
            w_lo(w1[:, at], 0)
            w_lo(an, 1)
            powers(1)
            norm_stats(0, stage)
            powers(2)
            norm_apply(0, stage)
            powers(3)
            w_lo(w1[:, wut], 2)
            w_lo(w1[:, wgt], 3)
            dve.wait_ge(ld_small, 48)
            dve.tensor_scalar(bias[:, 1, :], bias[:, 1, :], 0.5, None, ALU.mult).then_inc(bias_set, 1)
            x_lo(0)
            w_lo(w1[:, bt], 4)
            w_lo(ct, 5)
            norm_stats(1, stage)
            norm_apply(1, stage)
            gate(0, 0)
            gate(0, 1)
            norm_stats(2, stage)
            x_lo(1)
            v_lo(0)
            norm_apply(2, stage)
            step(0)
            with dve.Fori(1, STEPS - 3) as j:
                step(j)
            step(STEPS - 3)
            dve.wait_ge(ffhi_set, 1)
            dve.tensor_tensor(w_gu[:, LO, :, 0:HIDDEN], raw_gu[:, :, :], w_gu[:, HI, :, 0:HIDDEN].bitcast(F32),
                              ALU.subtract).then_inc(fflo_set, 1)
            step(STEPS - 2)
            dve.wait_ge(ffhi_set, 2)
            dve.tensor_tensor(w_dn[:, LO, :, :], raw_dn, w_dn[:, HI, :, :].bitcast(F32),
                              ALU.subtract).then_inc(fflo_set, 1)
            dve.wait_ge(ffhi_set, 3)
            dve.tensor_tensor(w_gu[:, LO, :, HIDDEN:], raw_gu[:, :, :], w_gu[:, HI, :, HIDDEN:].bitcast(F32),
                              ALU.subtract).then_inc(fflo_set, 1)
            step(STEPS - 1)
            add_tokens(STEPS - 1, y_done, y_added)

            dve.memset(start[:, :, :, 0], 0.0).then_inc(zero_set, 1)
            dve.wait_ge(send_set, 2)
            ends = s_end.rearrange("p k (b c) -> p k b c", c=CHUNKS)
            dve.tensor_copy(start[:, :, :, 1], ends[:, :, :, 0]).then_inc(start_set, 1)

            def chunk(c):
                dve.wait_ge(bst_done, c)
                dve.tensor_tensor(start[:, :, :, c + 1],
                                  up_ps[:, 2, 0:KD * BATCH].rearrange("p (k b) -> p k b", k=KD),
                                  ends[:, :, :, c], ALU.add).then_inc(start_set, 1)

            def hm_lo(j):
                dve.wait_ge(hmhi_set, j + 1)
                dve.tensor_tensor(hm[:, j, LO, :, :], up_ps[:, 0, :].rearrange("p (k n) -> p k n", k=KD),
                                  hm[:, j, HI, :, :].bitcast(F32), ALU.subtract).then_inc(hmlo_set, 1)

            hm_lo(0)
            with dve.Fori(0, STEPS - 1) as r:
                chunk(2 * r + 1)
                chunk(2 * r + 2)
                hm_lo(r + 1)
            for k in range(KD):
                dve.wait_ge(starthi_set, k + 1)
                dve.tensor_tensor(sT[:, LO, k, :].rearrange("p (b c) -> p b c", c=CHUNKS), start[:, k, :, :],
                                  sT[:, HI, k, :].bitcast(F32).rearrange("p (b c) -> p b c", c=CHUNKS),
                                  ALU.subtract).then_inc(startlo_set, 1)
            dve.wait_ge(fflo_set, 3)
            dve.tensor_reduce(lo_max[:, 0:1], w_gu[:, LO, :, :].bitcast(F32), mybir.AxisListType.XY, ALU.max,
                              apply_absolute_value=True).then_inc(lomax_set, 1)
            dve.tensor_reduce(lo_max[:, 1:2], w_dn[:, LO, :, :].bitcast(F32), mybir.AxisListType.XY, ALU.max,
                              apply_absolute_value=True).then_inc(lomax_set, 1)
            dve.wait_ge(lomax_set, 2)
            dve.tensor_tensor(lo_max[:, 0:1], lo_max[:, 0:1], lo_max[:, 1:2], ALU.max).then_inc(lomax_set, 1)
            dve.wait_ge(loall_set, 1)
            dve.tensor_scalar(wide[:, :], lo_all[:, :], 0.0, None, ALU.is_gt).then_inc(wide_set, 1)

            def hid_mul(j, m):
                dve.wait_ge(silu_set, KH * j + m + 1)
                if m >= 2 or inside(j, 1, STEPS):
                    dve.wait_ge(hlo_set, KH * j + m - 1)
                dve.tensor_tensor(hid[:, m % 2, :], up_ps[:, 2 * (m % 2) + 1, :], silu[:, m % 2, :],
                                  ALU.mult).then_inc(hid_set, 1)

            def add_down(j):
                dve.wait_ge(dn_done, KH * (j + 1))
                for b in range(2):
                    half = hres[:, bass.ds(j * GROUPS + 2 * b, 2), :]
                    dve.scalar_tensor_tensor(out=half, in0=dn_ps[:, b, :, :], scalar=SCALE * SCALE, in1=half,
                                             op0=ALU.mult, op1=ALU.add).then_inc(out_set, 1)

            def corrected(j):
                add_tokens(j, corr_done, h2_set)
                wait_alone(dve, h2_set, 2 * j + 2)
                norm_stats(STEPS + j, hres)

            def step_2(j):
                hid_mul(j, 0)
                if inside(j, 1, STEPS):
                    add_down(j - 1)
                hid_mul(j, 1)
                hid_mul(j, 2)
                if inside(j, 0, STEPS - 1):
                    corrected(j + 1)
                hid_mul(j, 3)
                hid_mul(j, 4)
                if inside(j, 0, STEPS - 1):
                    norm_apply(STEPS + j + 1, hres)
                hid_mul(j, 5)
                if inside(j, 0, STEPS - 1):
                    x_lo(STEPS + j + 1)

            corrected(0)
            norm_apply(STEPS, hres)
            x_lo(STEPS)
            step_2(0)
            with dve.Fori(1, STEPS - 1) as j:
                step_2(j)
            step_2(STEPS - 1)
            add_down(STEPS - 1)


def kernel(**inputs):
    import numpy as np
    import concourse.bacc as bacc
    from concourse.bass_utils import run_bass_kernel_spmd

    get = {k: np.asarray(val) for k, val in inputs.items()}
    arrays = {
        "x": get["x"].reshape(-1),
        "table": get["L0_tok_W"].T,
        "wu": get["L0_attn_W_u"].T, "bu": get["L0_attn_b_u"],
        "wg": get["L0_attn_W_g"].T, "bg": get["L0_attn_b_g"],
        "a_t": get["L0_attn_A"].T, "a_n": get["L0_attn_A"],
        "bm": get["L0_attn_Bm"].T, "cm": get["L0_attn_Cm"].T, "d": get["L0_attn_D"],
        "w_gate": get["L0_ffn_w_gate"].T, "w_up": get["L0_ffn_w_up"].T, "w_down": get["L0_ffn_w_down"].T,
    }
    arrays = {k: np.ascontiguousarray(val) for k, val in arrays.items()}
    nc = bacc.Bacc("TRN2", target_bir_lowering=False, num_devices=1)
    args = [nc.dram_tensor(k, val.shape, mybir.dt.from_np(val.dtype), kind="ExternalInput").ap()
            for k, val in arrays.items()]
    out = nc.dram_tensor("out", (BATCH * SEQ, DIM), F32, kind="ExternalOutput").ap()
    build(nc, *args, out)
    r = run_bass_kernel_spmd(nc, [arrays], core_ids=[0])
    return r.results[0]["out"].reshape(BATCH, SEQ, DIM)
```

```python
from contextlib import ExitStack

import concourse.bass as bass
from concourse import mybir

F32 = mybir.dt.float32
F32R = mybir.dt.float32r
I32 = mybir.dt.int32
ALU = mybir.AluOpType
ACT = mybir.ActivationFunctionType

P = 128
BATCH, SEQ, DIM = 16, 512, 256
STEPS = 16
CHUNKS = SEQ // STEPS
COLS = BATCH * CHUNKS
GROUPS = COLS // P
KD = DIM // P
HIDDEN = 768
KH = HIDDEN // P
INNER = 4
OUTER = CHUNKS // INNER
HM_LEFT = 2 * (INNER - 1) + OUTER - 1
FF_PARTS = 6
HI, LO = 0, 1
SCALE = 1.0 / 127.0
EPS = 1e-5
SPLIT = ((HI, HI), (HI, LO), (LO, HI))
H_SLOTS = 3


def build(nc, x, table, wu, bu, wg, bg, a_t, a_n, bm, cm, d, w_gate, w_up, w_down, out):
    ctx = ExitStack()
    phase1 = ExitStack()
    phase2 = ExitStack()
    with ctx:
        def sb(name, shape, dt, stack=ctx):
            return stack.enter_context(nc.sbuf_tensor(name, shape, dt))

        def sem(name):
            return ctx.enter_context(nc.semaphore(name))

        hres = sb("hres", [P, STEPS * GROUPS, DIM], F32)
        w_ff = sb("w_ff", [P, 2, FF_PARTS * HIDDEN], F32R)
        xn = sb("xn", [P, GROUPS, DIM], F32)
        xT = sb("xT", [P, 2, KD, COLS], F32R)
        sT = sb("sT", [P, 2, KD, COLS], F32R)
        split12 = sb("split12", [P, 12 * DIM], F32R)
        work8 = sb("work8", [P, 4, COLS], F32)
        ident = sb("ident", [P, P], F32)
        bias = sb("bias", [P, 2, KD], F32)
        bn = sb("bn", [P, GROUPS, 6], F32)
        mv = sb("mv", [P, GROUPS, 2], F32)
        var_eps = sb("var_eps", [P, GROUPS], F32)
        rstd = sb("rstd", [P, GROUPS], F32)
        neg_half = sb("neg_half", [P, GROUPS], F32)
        lo_max = sb("lo_max", [P, FF_PARTS + 1], F32)
        lo_all = sb("lo_all", [P, 1], F32)
        wide = sb("wide", [P, 1], I32)
        m16 = sb("m16", [P, KD, DIM], F32)

        w_gu = w_ff[:, :, 0:4 * HIDDEN].rearrange("p s (k n) -> p s k n", k=KD)
        w_dn = w_ff[:, :, 4 * HIDDEN:].rearrange("p s (k n) -> p s k n", k=KH)
        an, an2, ct = (split12[:, n * 4 * DIM:(n + 1) * 4 * DIM].rearrange("p (s k n) -> p s k n", s=2, k=KD)
                       for n in range(3))
        hT = split12[:, :].rearrange("p (m s n) -> p m s n", m=H_SLOTS, s=2)
        s_end = work8[:, 0:2, :]
        start = work8[:, 2:4, :]
        ends_i = s_end.rearrange("p k (bq i) -> p k i bq", i=INNER)
        start_i = start.rearrange("p k (bq i) -> p k i bq", i=INNER)
        start_q = start.rearrange("p k (b q i) -> p k i q b", q=OUTER, i=INNER)[:, :, 0]
        m64 = xn[:, 0:2, :]
        group_end = xn[:, 2, :].rearrange("p (k bq) -> p k bq", k=KD)
        group_end_q = xn[:, 2, :].rearrange("p (k b q) -> p k q b", k=KD, q=OUTER)
        silu = work8[:, 0:2, :]
        hid = work8[:, 2:4, :]

        raw = sb("raw", [P, 6, KD, DIM], F32, phase1)
        w1 = sb("w1", [P, 4, 2, KD, DIM], F32R, phase1)
        stage = sb("stage", [P, 2, GROUPS, DIM], F32, phase1)
        idx_t = sb("idx_t", [P, 2, GROUPS], I32, phase1)
        idx = sb("idx", [P, GROUPS, STEPS], I32, phase1)
        d_row = sb("d_row", [P, DIM], F32, phase1)
        acts = sb("acts", [P, 4, COLS], F32, phase1)
        v = sb("v", [P, KD, COLS], F32, phase1)
        vT = sb("vT", [P, 2, KD, COLS], F32R, phase1)
        raw_gu = sb("raw_gu", [P, KD, HIDDEN], I32, phase1)
        gelu, tanh = acts[:, 0:2, :], acts[:, 2:4, :]
        early = hres[:, (STEPS - 3) * GROUPS:, :].rearrange("p (b s k) n -> p b s k n", b=3, s=2)
        powers_of_a = [(raw[:, 0], raw[:, 1]), (early[:, 0, 0], early[:, 0, 1]), (early[:, 1, 0], early[:, 1, 1]),
                       (early[:, 2, 0], early[:, 2, 1]), (m16[:, :, :], raw[:, 3]), (raw[:, 4], raw[:, 5]), (m64, None)]
        raw_dn = raw[:, 0:3, :, :].rearrange("p a k n -> p (a k) n").bitcast(I32)
        at, wut, wgt, bt = 0, 1, 2, 3
        phase1.close()
        hm = sb("hm", [P, STEPS, 2, KD, DIM], F32R, phase2)
        phase2.close()

        xt_ps = ctx.enter_context(nc.psum_tensor("xt_ps", [P, 2, COLS], F32))
        up_ps = ctx.enter_context(nc.psum_tensor("up_ps", [P, 4, COLS], F32))
        st_ps = ctx.enter_context(nc.psum_tensor("st_ps", [P, 2, COLS], F32))
        tok_ps = xt_ps[:, :, :].rearrange("p b (g n) -> p b g n", n=DIM)
        dn_ps = st_ps[:, :, :].rearrange("p b (g n) -> p b g n", n=DIM)

        ld_idx, ld_a, ld_ug, ld_w, ld_small, ld_gu, ld_dn = (
            sem(n) for n in ("ld_idx", "ld_a", "ld_ug", "ld_w", "ld_small", "ld_gu", "ld_dn"))
        gathered = [sem("gathered0"), sem("gathered1")]
        idx_set = sem("idx_set")
        const_set = sem("const_set")
        ident_set = sem("ident_set")
        rows_in = sem("rows_in")
        hres_set = sem("hres_set")
        bn_set = sem("bn_set")
        mv_set = sem("mv_set")
        eps_set = sem("eps_set")
        rstd_set = sem("rstd_set")
        xn_set = sem("xn_set")
        xt_done = sem("xt_done")
        xhi_set = sem("xhi_set")
        xlo_set = sem("xlo_set")
        whi_set = sem("whi_set")
        wlo_set = sem("wlo_set")
        ffhi_set = sem("ffhi_set")
        fflo_set = sem("fflo_set")
        lomax_set = sem("lomax_set")
        loall_set = sem("loall_set")
        wide_set = sem("wide_set")
        bias_set = sem("bias_set")
        pow_done = sem("pow_done")
        pow_set = sem("pow_set")
        ug_done = sem("ug_done")
        act_set = sem("act_set")
        v_set = sem("v_set")
        vhi_set = sem("vhi_set")
        vlo_set = sem("vlo_set")
        bv_done = sem("bv_done")
        s_done = sem("s_done")
        shi_set = sem("shi_set")
        slo_set = sem("slo_set")
        y_done = sem("y_done")
        y_added = sem("y_added")
        send_set = sem("send_set")
        zero_set = sem("zero_set")
        start_set = sem("start_set")
        bst_done = sem("bst_done")
        hm_done = sem("hm_done")
        hmhi_set = sem("hmhi_set")
        hmlo_set = sem("hmlo_set")
        starthi_set = sem("starthi_set")
        startlo_set = sem("startlo_set")
        corr_done = sem("corr_done")
        h2_set = sem("h2_set")
        gu_done = sem("gu_done")
        silu_set = sem("silu_set")
        hid_set = sem("hid_set")
        hhi_set = sem("hhi_set")
        hlo_set = sem("hlo_set")
        dn_done = sem("dn_done")
        out_set = sem("out_set")
        stored = sem("stored")

        block = ctx.enter_context(nc.Block())
        out_v = out.rearrange("(g p j) d -> p g j d", p=P, j=STEPS)

        def inside(t, first, end):
            return first <= t < end if isinstance(t, int) else True

        carrier = {e.engine: e.alloc_register("wait_carrier") for e in (nc.vector, nc.gpsimd)}

        def wait_alone(eng, semaphore, count):
            if not isinstance(count, int):
                eng.reg_add(carrier[eng.engine], count, 0)
                count = carrier[eng.engine]
            eng.wait_ge(const_set, 2)
            eng.wait_ge(semaphore, count)

        def tiles(t):
            return hres[:, bass.ds(t * GROUPS, GROUPS), :]

        @block.sync
        def _(sp):
            sp.dma_start(idx[:, :, :], x.rearrange("(g p j) -> p g j", p=P, j=STEPS)).then_inc(ld_idx, 16)
            def load(n, w, loaded):
                sp.dma_start(raw[:, n, :, :], w.rearrange("(k p) n -> p k n", p=P)).then_inc(loaded, 16)

            load(0, a_t, ld_a)
            load(1, a_n, ld_a)
            load(2, wu, ld_ug)
            load(3, wg, ld_ug)
            sp.dma_start(d_row[:, :], d.partition_broadcast(P)).then_inc(ld_small, 16)
            with nc.allow_non_contiguous_dma("two vectors of 256 values"):
                sp.dma_start(bias[:, 0, :], bu.rearrange("(k p) -> p k", p=P)).then_inc(ld_small, 16)
                sp.dma_start(bias[:, 1, :], bg.rearrange("(k p) -> p k", p=P)).then_inc(ld_small, 16)
            load(4, bm, ld_w)
            load(5, cm, ld_w)
            sp.dma_start(raw_gu[:, :, :], w_gate.rearrange("(k p) n -> p k n", p=P)).then_inc(ld_gu, 16)
            sp.wait_ge(whi_set, 6)
            sp.wait_ge(wlo_set, 6)
            sp.wait_ge(pow_done, 2)
            sp.dma_start(raw_dn, w_down.rearrange("(k p) n -> p k n", p=P)).then_inc(ld_dn, 16)
            sp.wait_ge(fflo_set, 1)
            sp.dma_start(raw_gu[:, :, :], w_up.rearrange("(k p) n -> p k n", p=P)).then_inc(ld_gu, 16)
            with sp.Fori(0, STEPS) as j:
                sp.wait_ge(out_set, 2 * j + 2)
                sp.dma_start(out_v[:, :, j, :], tiles(j)).then_inc(stored, 16)
            sp.wait_ge(stored, 16 * STEPS)

        @block.gpsimd
        def _(pool):
            pool.memset(ident[:, :], 0.0).then_inc(const_set, 1)
            pool.memset(neg_half[:, :], -0.5).then_inc(const_set, 1)
            pool.wait_ge(const_set, 2)
            pool.affine_select(out=ident[:, :], in_=ident[:, :], compare_op=ALU.not_equal, fill=1.0, base=0,
                               pattern=[[-1, P]], channel_multiplier=1).then_inc(ident_set, 1)
            pool.wait_ge(ld_idx, 16)

            def gather(j, p):
                pool.tensor_copy(idx_t[:, p, :], idx[:, :, j]).then_inc(idx_set, 1)
                wait_alone(pool, idx_set, j + 1)
                for g in range(GROUPS):
                    pool.indirect_dma_start(
                        out=stage[:, p, g, :], out_offset=None, in_=table,
                        in_offset=bass.IndirectOffsetOnAxis(ap=idx_t[:, p, g:g + 1], axis=0),
                    ).then_inc(gathered[p], 16)

            def rstd_of(n):
                wait_alone(pool, mv_set, n + 1)
                pool.tensor_scalar(var_eps[:, :], mv[:, :, 1], EPS, None, ALU.add).then_inc(eps_set, 1)
                pool.wait_ge(eps_set, n + 1)
                pool.tensor_tensor(rstd[:, :], var_eps[:, :], neg_half[:, :], ALU.pow).then_inc(rstd_set, 1)

            gather(0, 0)
            gather(1, 1)
            pool.wait_ge(ld_small, 48)

            def tile_in(j, p, n_even, more):
                pool.wait_ge(gathered[p], (n_even + 1) * GROUPS * 16)
                pool.sem_inc(rows_in, 1)
                pool.tensor_tensor(tiles(j), stage[:, p, :, :],
                                   d_row[:, None, :].to_broadcast([P, GROUPS, DIM]), ALU.add).then_inc(hres_set, 1)
                rstd_of(j)
                if more:
                    pool.wait_ge(xn_set, j + 1)
                    pool.wait_ge(hres_set, j + 1)
                    gather(j + 2, p)

            with pool.Fori(0, STEPS // 2 - 1) as i:
                tile_in(2 * i, 0, i, True)
                tile_in(2 * i + 1, 1, i, True)
            tile_in(STEPS - 2, 0, STEPS // 2 - 1, False)
            tile_in(STEPS - 1, 1, STEPS // 2 - 1, False)

            pool.wait_ge(ld_gu, 16)
            pool.tensor_copy(w_gu[:, HI, :, 0:HIDDEN], raw_gu[:, :, :]).then_inc(ffhi_set, 1)
            pool.wait_ge(ld_dn, 16)
            pool.tensor_copy(w_dn[:, HI, :, :], raw_dn).then_inc(ffhi_set, 1)
            pool.wait_ge(ld_gu, 32)
            pool.tensor_copy(w_gu[:, HI, :, HIDDEN:], raw_gu[:, :, :]).then_inc(ffhi_set, 1)
            pool.wait_ge(lomax_set, FF_PARTS + 1)
            pool.partition_all_reduce(lo_all[:, :], lo_max[:, FF_PARTS:], P, bass.bass_isa.ReduceOp.max).then_inc(loall_set, 1)

            with pool.Fori(STEPS, 2 * STEPS) as n:
                rstd_of(n)

        @block.tensor
        def _(pe):
            def product(ps, w, m, r, first=True, last=True):
                n = 0
                for k in range(KD):
                    for ws, rs in SPLIT:
                        mm = pe.matmul(ps, w[:, ws, k, m * P:(m + 1) * P], r[:, rs, k, :],
                                       start=first and n == 0, stop=last and n == KD * len(SPLIT) - 1)
                        n += 1
                return mm

            def transposes(n):
                pe.wait_ge(xn_set, n + 1)
                for k in range(KD):
                    for g in range(GROUPS):
                        t = pe.transpose(xt_ps[:, k, g * P:(g + 1) * P], xn[:, g, k * P:(k + 1) * P], ident[:, :])
                    t.then_inc(xt_done, 1)

            def tokens(w, r, done):
                for b in range(2):
                    for g in range(2):
                        n = 0
                        for k in range(KD):
                            for ws, rs in SPLIT:
                                c = (2 * b + g) * P
                                mm = pe.matmul(tok_ps[:, b, g, :], w[:, ws, k, c:c + P], r[:, rs, k, :],
                                               start=n == 0, stop=n == KD * len(SPLIT) - 1)
                                n += 1
                    mm.then_inc(done, 1)

            def power(r, banks):
                if r == 0:
                    pe.wait_ge(ld_a, 32)
                else:
                    pe.wait_ge(pow_set, 2 * r)
                flipped, plain = powers_of_a[r]
                for side in range(2 if r < 5 else 1):
                    w, moving = (plain, flipped) if side == 0 else (flipped, plain)
                    for m in range(KD):
                        for k in range(KD):
                            mm = pe.matmul(banks[:, side, m * DIM:(m + 1) * DIM],
                                           w[:, k, m * P:(m + 1) * P], moving[:, k, :], start=k == 0, stop=k == KD - 1)
                    mm.then_inc(pow_done, 1)

            def ug(j, m):
                pe.wait_ge(xlo_set, 2 * j + 2)
                if inside(j, 1, STEPS):
                    pe.wait_ge(act_set, 2 * j + m - 1)
                product(up_ps[:, 2 * m, :], w1[:, wut], m, xT)
                product(up_ps[:, 2 * m + 1, :], w1[:, wgt], m, xT).then_inc(ug_done, 1)

            def states(j):
                pe.wait_ge(vlo_set, 2 * j + 2)
                if inside(j, 1, STEPS):
                    pe.wait_ge(slo_set, 2 * j)
                else:
                    pe.wait_ge(wlo_set, 6)
                    pe.wait_ge(pow_set, 8)
                for m in range(KD):
                    mm = product(st_ps[:, m, :], w1[:, bt], m, vT, last=not inside(j, 1, STEPS))
                    if not inside(j, 1, STEPS):
                        mm.then_inc(s_done, 1)
                if not inside(j, 1, STEPS):
                    return
                mm.then_inc(bv_done, 1)
                for m in range(KD):
                    product(st_ps[:, m, :], w1[:, at], m, sT, first=False).then_inc(s_done, 1)

            def outputs(j):
                pe.wait_ge(slo_set, 2 * j + 2)
                pe.wait_ge(xlo_set, min(2 * (j + 3), 2 * STEPS) if isinstance(j, int) else 2 * (j + 3))
                if inside(j, 1, STEPS):
                    pe.wait_ge(y_added, 2 * j)
                tokens(sT, ct, y_done)

            def step(j):
                if inside(j, 0, STEPS - 1):
                    ug(j + 1, 0)
                if inside(j, 1, STEPS):
                    outputs(j - 1)
                if inside(j, 0, STEPS - 1):
                    ug(j + 1, 1)
                if inside(j, 0, STEPS - 2):
                    if inside(j, 1, STEPS):
                        pe.wait_ge(y_added, 2 * j)
                    else:
                        pe.wait_ge(xlo_set, 4)
                    transposes(j + 2)
                states(j)

            power(0, st_ps)
            power(1, st_ps)
            pe.wait_ge(ident_set, 1)
            transposes(0)
            pe.wait_ge(wlo_set, 2)
            ug(0, 0)
            ug(0, 1)
            power(2, st_ps)
            transposes(1)
            power(3, st_ps)
            step(0)
            with pe.Fori(1, STEPS - 2) as j:
                step(j)
            step(STEPS - 2)
            pe.wait_ge(act_set, 2 * STEPS)
            power(4, up_ps[:, 0:2, :])
            step(STEPS - 1)
            power(5, up_ps[:, 2:4, :])
            outputs(STEPS - 1)

            def hm_product(j, w, r):
                for m in range(KD):
                    mm = product(up_ps[:, j % 2, m * DIM:(m + 1) * DIM], w, m, r)
                mm.then_inc(hm_done, 1)

            def hm_next(j):
                pe.wait_ge(hmlo_set, j - 1)
                hm_product(j, an2, hm[:, j - 2])

            def boundary(matrix, state, cols, count):
                pe.wait_ge(start_set, count)
                for m in range(KD):
                    for k in range(KD):
                        mm = pe.matmul(st_ps[:, 0, m * cols:(m + 1) * cols], matrix[:, k, m * P:(m + 1) * P],
                                       state(k), start=k == 0, stop=k == KD - 1)
                mm.then_inc(bst_done, 1)

            hm_product(0, an, ct)
            boundary(m16, lambda k: start_i[:, k, 1, :], BATCH * OUTER, 1)
            pe.wait_ge(hmlo_set, 1)
            hm_product(1, an, hm[:, 0])
            with pe.Fori(2, INNER) as i:
                boundary(m16, lambda k: start_i[:, k, i, :], BATCH * OUTER, i)
                hm_next(i)
            pe.wait_ge(pow_set, 11)
            with pe.Fori(1, OUTER - 1) as q:
                boundary(m64, lambda k: start_q[:, k, q, :], BATCH, q + INNER)
                hm_next(q + INNER - 1)
            with pe.Fori(0, INNER - 1) as i:
                boundary(m16, lambda k: start_i[:, k, i, :], BATCH * OUTER, i + OUTER + INNER - 1)
                hm_next(i + OUTER + INNER - 2)
            hm_next(HM_LEFT)

            def corrections(j):
                tokens(sT, hm[:, j], corr_done)

            def phase_2(lo_weights):
                parts = ((HI, HI), (HI, LO), (LO, HI)) if lo_weights else ((HI, HI), (HI, LO))

                def gate_up(j, m):
                    if m == 0:
                        pe.wait_ge(xlo_set, 2 * (j + STEPS) + 2)
                    if m >= 2 or inside(j, 1, STEPS):
                        pe.wait_ge(hid_set, KH * j + m - 1)
                    for side in range(2):
                        n = 0
                        for k in range(KD):
                            for ws, rs in parts:
                                c = side * HIDDEN + m * P
                                mm = pe.matmul(up_ps[:, 2 * (m % 2) + side, :], w_gu[:, ws, k, c:c + P],
                                               xT[:, rs, k, :], start=n == 0, stop=n == KD * len(parts) - 1)
                                n += 1
                    mm.then_inc(gu_done, 1)

                def down(j, m):
                    pe.wait_ge(hlo_set, KH * j + m + 1)
                    if m == 0 and inside(j, 1, STEPS):
                        pe.wait_ge(out_set, 2 * j)
                    for g in range(GROUPS):
                        for n, (ws, hs) in enumerate(parts):
                            mm = pe.matmul(dn_ps[:, g // 2, g % 2, :],
                                           hT[:, m % H_SLOTS, hs, g * P:(g + 1) * P], w_dn[:, ws, m, :],
                                           start=m == 0 and g % 2 == 0 and n == 0,
                                           stop=m == KH - 1 and n == len(parts) - 1, skip_group_check=True)
                    mm.then_inc(dn_done, 1)

                def step_2(j):
                    gate_up(j, 0)
                    if inside(j, 0, STEPS - 1):
                        corrections(j + 1)
                    if inside(j, 1, STEPS):
                        down(j - 1, KH - 2)
                    gate_up(j, 1)
                    if inside(j, 1, STEPS):
                        down(j - 1, KH - 1)
                    gate_up(j, 2)
                    gate_up(j, 3)
                    down(j, 0)
                    gate_up(j, 4)
                    if inside(j, 0, STEPS - 1):
                        transposes(STEPS + j + 1)
                    gate_up(j, 5)
                    down(j, 1)
                    down(j, 2)
                    down(j, 3)

                step_2(0)
                with pe.Fori(1, STEPS - 1) as j:
                    step_2(j)
                step_2(STEPS - 1)
                down(STEPS - 1, KH - 2)
                down(STEPS - 1, KH - 1)

            pe.wait_ge(startlo_set, 2)
            pe.wait_ge(y_added, 2 * STEPS)
            corrections(0)
            with pe.Fori(HM_LEFT + 1, STEPS) as j:
                hm_next(j)
            pe.wait_ge(hmlo_set, STEPS)
            pe.wait_ge(h2_set, 2)
            transposes(STEPS)
            pe.wait_ge(wide_set, 1)
            pe.wait_ge(fflo_set, 3)
            is_wide = pe.value_load(wide[0:1, 0:1], min_val=0, max_val=1)
            with pe.If(is_wide == 0):
                phase_2(False)
            with pe.Else():
                phase_2(True)

        @block.scalar
        def _(act):
            def w_hi(dst, n):
                act.activation(dst[:, HI], raw[:, n, :, :], ACT.Copy).then_inc(whi_set, 1)

            act.preload_act_table(ACT.Gelu)
            act.wait_ge(ld_ug, 32)
            w_hi(w1[:, wut], 2)
            w_hi(w1[:, wgt], 3)
            act.wait_ge(ld_a, 32)
            w_hi(w1[:, at], 0)
            w_hi(an, 1)
            act.wait_ge(ld_w, 32)
            w_hi(w1[:, bt], 4)
            w_hi(ct, 5)
            act.wait_ge(pow_set, 2)
            act.activation(an2[:, HI], powers_of_a[1][1], ACT.Copy).then_inc(whi_set, 1)

            def x_hi(n):
                for k in range(KD):
                    act.wait_ge(xt_done, 2 * n + k + 1)
                    act.activation(xT[:, HI, k, :], xt_ps[:, k, :], ACT.Copy).then_inc(xhi_set, 1)

            def gates(j, m):
                act.wait_ge(ug_done, 2 * j + m + 1)
                if inside(j, 1, STEPS):
                    act.wait_ge(v_set, 2 * j + m - 1)
                act.activation(gelu[:, m, :], up_ps[:, 2 * m, :], ACT.Gelu, bias=bias[:, 0, m:m + 1])
                act.activation(tanh[:, m, :], up_ps[:, 2 * m + 1, :], ACT.Tanh, bias=bias[:, 1, m:m + 1],
                               scale=0.5).then_inc(act_set, 1)

            def v_hi(j):
                if inside(j, 1, STEPS):
                    if isinstance(j, int) and j == 1:
                        act.wait_ge(s_done, 2)
                    else:
                        act.wait_ge(bv_done, j - 1)
                for m in range(KD):
                    act.wait_ge(v_set, 2 * j + m + 1)
                    act.activation(vT[:, HI, m, :], v[:, m, :], ACT.Copy).then_inc(vhi_set, 1)

            def s_hi(j):
                act.wait_ge(s_done, 2 * j + 2)
                for m in range(KD):
                    act.activation(sT[:, HI, m, :], st_ps[:, m, :], ACT.Copy).then_inc(shi_set, 1)

            def step(j):
                if inside(j, 0, STEPS - 1):
                    gates(j + 1, 0)
                    gates(j + 1, 1)
                if inside(j, 0, STEPS - 2):
                    x_hi(j + 2)
                if inside(j, 0, STEPS - 1):
                    v_hi(j + 1)
                s_hi(j)

            x_hi(0)
            act.wait_ge(bias_set, 1)
            gates(0, 0)
            gates(0, 1)
            x_hi(1)
            v_hi(0)
            step(0)
            with act.Fori(1, STEPS - 2) as j:
                step(j)
            step(STEPS - 2)
            step(STEPS - 1)
            for m in range(KD):
                act.wait_ge(slo_set, 2 * STEPS - 1 + m)
                act.activation(s_end[:, m, :], st_ps[:, m, :], ACT.Copy).then_inc(send_set, 1)

            def hm_hi(j):
                act.wait_ge(hm_done, j + 1)
                act.activation(hm[:, j, HI, :, :], up_ps[:, j % 2, :].rearrange("p (k n) -> p k n", k=KD),
                               ACT.Copy).then_inc(hmhi_set, 1)

            act.preload_act_table(ACT.Silu)
            with act.Fori(0, HM_LEFT) as j:
                hm_hi(j)
            act.wait_ge(start_set, 2 * INNER + OUTER - 2)
            act.wait_ge(y_done, 2 * STEPS)
            act.wait_ge(zero_set, 1)
            for k in range(KD):
                act.activation(sT[:, HI, k, :], start[:, k, :], ACT.Copy).then_inc(starthi_set, 1)
            with act.Fori(HM_LEFT, STEPS) as j:
                hm_hi(j)

            def silu_of(j, m):
                act.wait_ge(gu_done, KH * j + m + 1)
                if m >= 2 or inside(j, 1, STEPS):
                    act.wait_ge(hid_set, KH * j + m - 1)
                act.activation(silu[:, m % 2, :], up_ps[:, 2 * (m % 2), :], ACT.Silu,
                               scale=SCALE).then_inc(silu_set, 1)

            def hid_hi(j, m):
                act.wait_ge(hid_set, KH * j + m + 1)
                if m >= H_SLOTS or inside(j, 1, STEPS):
                    act.wait_ge(dn_done, KH * j + m + 1 - H_SLOTS)
                act.activation(hT[:, m % H_SLOTS, HI, :], hid[:, m % 2, :], ACT.Copy).then_inc(hhi_set, 1)

            def step_2(j):
                for m in range(KH - 1):
                    silu_of(j, m)
                    if m > 0:
                        hid_hi(j, m - 1)
                if inside(j, 0, STEPS - 1):
                    act.wait_ge(gu_done, KH * (j + 1))
                    x_hi(STEPS + j + 1)
                silu_of(j, KH - 1)
                hid_hi(j, KH - 2)
                hid_hi(j, KH - 1)

            x_hi(STEPS)
            step_2(0)
            with act.Fori(1, STEPS - 1) as j:
                step_2(j)
            step_2(STEPS - 1)

        @block.vector
        def _(dve):
            w_order = (2, 3, 0, 1, 4, 5)

            def w_lo(dst, n):
                dve.wait_ge(whi_set, w_order.index(n) + 1)
                dve.tensor_tensor(dst[:, LO], raw[:, n, :, :], dst[:, HI].bitcast(F32),
                                  ALU.subtract).then_inc(wlo_set, 1)

            def norm_stats(n, src):
                if isinstance(n, int) and n < 2:
                    dve.wait_ge(gathered[n], GROUPS * 16)
                elif src is stage:
                    wait_alone(dve, rows_in, n + 1)
                for g in range(GROUPS):
                    rows = stage[:, n % 2, g, :] if src is stage else hres[:, (n - STEPS) * GROUPS + g, :]
                    last = dve.bn_stats(bn[:, g, :], rows)
                last.then_inc(bn_set, 1)
                wait_alone(dve, bn_set, n + 1)
                for g in range(GROUPS):
                    last = dve.bn_aggr(mv[:, g, :], bn[:, g, :])
                last.then_inc(mv_set, 1)

            def norm_apply(n, src):
                dve.wait_ge(rstd_set, n + 1)
                if not (isinstance(n, int) and n == 0):
                    dve.wait_ge(xt_done, 2 * n)
                for g in range(GROUPS):
                    rows = stage[:, n % 2, g, :] if src is stage else hres[:, (n - STEPS) * GROUPS + g, :]
                    last = dve.tensor_scalar(xn[:, g, :], rows, mv[:, g, 0:1], rstd[:, g:g + 1],
                                             ALU.subtract, ALU.mult)
                last.then_inc(xn_set, 1)

            def x_lo(n):
                for k in range(KD):
                    dve.wait_ge(xhi_set, 2 * n + k + 1)
                    dve.tensor_tensor(xT[:, LO, k, :], xt_ps[:, k, :], xT[:, HI, k, :].bitcast(F32),
                                      ALU.subtract).then_inc(xlo_set, 1)

            def gate(j, m):
                dve.wait_ge(act_set, 2 * j + m + 1)
                if inside(j, 1, STEPS):
                    dve.wait_ge(vlo_set, 2 * j + m - 1)
                dve.scalar_tensor_tensor(out=v[:, m, :], in0=tanh[:, m, :], scalar=1.0, in1=gelu[:, m, :],
                                         op0=ALU.add, op1=ALU.mult).then_inc(v_set, 1)

            def v_lo(j):
                for m in range(KD):
                    dve.wait_ge(vhi_set, 2 * j + m + 1)
                    dve.tensor_tensor(vT[:, LO, m, :], v[:, m, :], vT[:, HI, m, :].bitcast(F32),
                                      ALU.subtract).then_inc(vlo_set, 1)

            def s_lo(j):
                for m in range(KD):
                    dve.wait_ge(shi_set, 2 * j + m + 1)
                    dve.tensor_tensor(sT[:, LO, m, :], st_ps[:, m, :], sT[:, HI, m, :].bitcast(F32),
                                      ALU.subtract).then_inc(slo_set, 1)

            def add_tokens(j, done, added):
                for b in range(2):
                    dve.wait_ge(done, 2 * j + b + 1)
                    half = hres[:, bass.ds(j * GROUPS + 2 * b, 2), :]
                    dve.scalar_tensor_tensor(out=half, in0=tok_ps[:, b, :, :], scalar=0.5, in1=half,
                                             op0=ALU.mult, op1=ALU.add).then_inc(added, 1)

            def step(j):
                if inside(j, 0, STEPS - 1):
                    gate(j + 1, 0)
                if inside(j, 1, STEPS):
                    add_tokens(j - 1, y_done, y_added)
                if inside(j, 0, STEPS - 1):
                    gate(j + 1, 1)
                if inside(j, 0, STEPS - 3):
                    norm_stats(j + 3, stage)
                if inside(j, 0, STEPS - 2):
                    x_lo(j + 2)
                if inside(j, 0, STEPS - 1):
                    v_lo(j + 1)
                s_lo(j)
                if inside(j, 0, STEPS - 3):
                    norm_apply(j + 3, stage)

            def powers(r, banks, sides=(0, 1)):
                for side in sides:
                    dve.wait_ge(pow_done, 2 * r + side + 1)
                    dve.tensor_copy(powers_of_a[r + 1][side], banks[:, side, :].rearrange("p (k n) -> p k n", k=KD)
                                    ).then_inc(pow_set, 1)

            w_lo(w1[:, wut], 2)
            w_lo(w1[:, wgt], 3)
            powers(0, st_ps, (0,))
            powers(0, st_ps, (1,))
            norm_stats(0, stage)
            norm_apply(0, stage)
            w_lo(w1[:, at], 0)
            w_lo(an, 1)
            dve.wait_ge(ld_small, 48)
            dve.tensor_scalar(bias[:, 1, :], bias[:, 1, :], 0.5, None, ALU.mult).then_inc(bias_set, 1)
            x_lo(0)
            norm_stats(1, stage)
            powers(1, st_ps)
            norm_apply(1, stage)
            w_lo(w1[:, bt], 4)
            w_lo(ct, 5)
            dve.wait_ge(whi_set, 7)
            dve.tensor_tensor(an2[:, LO], powers_of_a[1][1], an2[:, HI].bitcast(F32), ALU.subtract).then_inc(wlo_set, 1)
            gate(0, 0)
            gate(0, 1)
            powers(2, st_ps)
            x_lo(1)
            v_lo(0)
            powers(3, st_ps)
            norm_stats(2, stage)
            norm_apply(2, stage)
            step(0)
            with dve.Fori(1, STEPS - 3) as j:
                step(j)
            step(STEPS - 3)
            dve.wait_ge(ffhi_set, 1)
            dve.tensor_tensor(w_gu[:, LO, :, 0:HIDDEN], raw_gu[:, :, :], w_gu[:, HI, :, 0:HIDDEN].bitcast(F32),
                              ALU.subtract).then_inc(fflo_set, 1)
            step(STEPS - 2)
            dve.wait_ge(ffhi_set, 2)
            dve.tensor_tensor(w_dn[:, LO, :, :], raw_dn, w_dn[:, HI, :, :].bitcast(F32),
                              ALU.subtract).then_inc(fflo_set, 1)
            dve.wait_ge(ffhi_set, 3)
            dve.tensor_tensor(w_gu[:, LO, :, HIDDEN:], raw_gu[:, :, :], w_gu[:, HI, :, HIDDEN:].bitcast(F32),
                              ALU.subtract).then_inc(fflo_set, 1)
            powers(4, up_ps[:, 0:2, :])
            step(STEPS - 1)
            powers(5, up_ps[:, 2:4, :], (0,))

            dve.memset(start_q[:, :, 0, :], 0.0).then_inc(zero_set, 1)
            dve.wait_ge(send_set, 2)
            dve.tensor_copy(start_i[:, :, 1, :], ends_i[:, :, 0, :]).then_inc(start_set, 1)

            def boundary(dst, end, cols, count):
                dve.wait_ge(bst_done, count)
                dve.tensor_tensor(dst, st_ps[:, 0, 0:KD * cols].rearrange("p (k c) -> p k c", k=KD), end,
                                  ALU.add).then_inc(start_set, 1)

            def hm_lo(j):
                dve.wait_ge(hmhi_set, j + 1)
                dve.tensor_tensor(hm[:, j, LO, :, :], up_ps[:, j % 2, :].rearrange("p (k n) -> p k n", k=KD),
                                  hm[:, j, HI, :, :].bitcast(F32), ALU.subtract).then_inc(hmlo_set, 1)

            boundary(start_i[:, :, 2, :], ends_i[:, :, 1, :], BATCH * OUTER, 1)
            hm_lo(0)
            boundary(start_i[:, :, 3, :], ends_i[:, :, 2, :], BATCH * OUTER, 2)
            hm_lo(1)
            boundary(group_end, ends_i[:, :, INNER - 1, :], BATCH * OUTER, INNER - 1)
            dve.wait_ge(start_set, INNER)
            dve.tensor_copy(start_q[:, :, 1, :], group_end_q[:, :, 0, :]).then_inc(start_set, 1)
            hm_lo(2)
            add_tokens(STEPS - 1, y_done, y_added)
            dve.wait_ge(fflo_set, 3)
            with dve.Fori(1, OUTER - 1) as q:
                boundary(start_q[:, :, q + 1, :], group_end_q[:, :, q, :], BATCH, q + INNER - 1)
                hm_lo(q + INNER - 2)
                dve.tensor_reduce(lo_max[:, bass.ds(q - 1, 1)],
                                  w_ff[:, LO, bass.ds((q - 1) * HIDDEN, HIDDEN)].bitcast(F32),
                                  mybir.AxisListType.X, ALU.max, apply_absolute_value=True).then_inc(lomax_set, 1)
            with dve.Fori(0, INNER - 1) as i:
                boundary(start_i[:, :, i + 1, :], ends_i[:, :, i, :], BATCH * OUTER, i + INNER + OUTER - 2)
                hm_lo(i + INNER + OUTER - 3)
            hm_lo(HM_LEFT - 1)
            for k in range(KD):
                dve.wait_ge(starthi_set, k + 1)
                dve.tensor_tensor(sT[:, LO, k, :], start[:, k, :], sT[:, HI, k, :].bitcast(F32),
                                  ALU.subtract).then_inc(startlo_set, 1)
            hm_lo(HM_LEFT)
            dve.wait_ge(lomax_set, FF_PARTS)
            dve.tensor_reduce(lo_max[:, FF_PARTS:], lo_max[:, 0:FF_PARTS], mybir.AxisListType.X,
                              ALU.max).then_inc(lomax_set, 1)

            def hid_lo(j, m):
                dve.wait_ge(hhi_set, KH * j + m + 1)
                dve.tensor_tensor(hT[:, m % H_SLOTS, LO, :], hid[:, m % 2, :],
                                  hT[:, m % H_SLOTS, HI, :].bitcast(F32), ALU.subtract).then_inc(hlo_set, 1)

            def hid_mul(j, m):
                dve.wait_ge(silu_set, KH * j + m + 1)
                if m >= 2 or inside(j, 1, STEPS):
                    dve.wait_ge(hlo_set, KH * j + m - 1)
                dve.tensor_tensor(hid[:, m % 2, :], up_ps[:, 2 * (m % 2) + 1, :], silu[:, m % 2, :],
                                  ALU.mult).then_inc(hid_set, 1)

            def add_down(j):
                dve.wait_ge(dn_done, KH * (j + 1))
                for b in range(2):
                    half = hres[:, bass.ds(j * GROUPS + 2 * b, 2), :]
                    dve.scalar_tensor_tensor(out=half, in0=dn_ps[:, b, :, :], scalar=SCALE * SCALE, in1=half,
                                             op0=ALU.mult, op1=ALU.add).then_inc(out_set, 1)

            def corrected(j):
                add_tokens(j, corr_done, h2_set)
                wait_alone(dve, h2_set, 2 * j + 2)
                norm_stats(STEPS + j, hres)

            def step_2(j):
                hid_mul(j, 0)
                if inside(j, 0, STEPS - 1):
                    corrected(j + 1)
                for m in range(1, KH - 1):
                    hid_mul(j, m)
                    hid_lo(j, m - 1)
                    if m == 1 and inside(j, 1, STEPS):
                        add_down(j - 1)
                    if m == 2 and inside(j, 0, STEPS - 1):
                        norm_apply(STEPS + j + 1, hres)
                if inside(j, 0, STEPS - 1):
                    x_lo(STEPS + j + 1)
                hid_mul(j, KH - 1)
                hid_lo(j, KH - 2)
                hid_lo(j, KH - 1)

            corrected(0)
            with dve.Fori(HM_LEFT + 1, STEPS) as j:
                hm_lo(j)
            norm_apply(STEPS, hres)
            dve.wait_ge(loall_set, 1)
            dve.tensor_scalar(wide[:, :], lo_all[:, :], 0.0, None, ALU.is_gt).then_inc(wide_set, 1)
            x_lo(STEPS)
            step_2(0)
            with dve.Fori(1, STEPS - 1) as j:
                step_2(j)
            step_2(STEPS - 1)
            add_down(STEPS - 1)


def kernel(**inputs):
    import numpy as np
    import concourse.bacc as bacc
    from concourse.bass_utils import run_bass_kernel_spmd

    get = {k: np.asarray(val) for k, val in inputs.items()}
    arrays = {
        "x": get["x"].reshape(-1),
        "table": get["L0_tok_W"].T,
        "wu": get["L0_attn_W_u"].T, "bu": get["L0_attn_b_u"],
        "wg": get["L0_attn_W_g"].T, "bg": get["L0_attn_b_g"],
        "a_t": get["L0_attn_A"].T, "a_n": get["L0_attn_A"],
        "bm": get["L0_attn_Bm"].T, "cm": get["L0_attn_Cm"].T, "d": get["L0_attn_D"],
        "w_gate": get["L0_ffn_w_gate"].T, "w_up": get["L0_ffn_w_up"].T, "w_down": get["L0_ffn_w_down"].T,
    }
    arrays = {k: np.ascontiguousarray(val) for k, val in arrays.items()}
    nc = bacc.Bacc("TRN2", target_bir_lowering=False, num_devices=1)
    args = [nc.dram_tensor(k, val.shape, mybir.dt.from_np(val.dtype), kind="ExternalInput").ap()
            for k, val in arrays.items()]
    out = nc.dram_tensor("out", (BATCH * SEQ, DIM), F32, kind="ExternalOutput").ap()
    build(nc, *args, out)
    r = run_bass_kernel_spmd(nc, [arrays], core_ids=[0])
    return r.results[0]["out"].reshape(BATCH, SEQ, DIM)
```

```python
from contextlib import ExitStack

import concourse.bass as bass
from concourse import mybir

F32 = mybir.dt.float32
F32R = mybir.dt.float32r
I32 = mybir.dt.int32
ALU = mybir.AluOpType
ACT = mybir.ActivationFunctionType

P = 128
BATCH, SEQ, DIM = 16, 512, 256
STEPS = 16
PAIRS = STEPS // 2
CHUNKS = SEQ // STEPS
COLS = BATCH * CHUNKS
GROUPS = COLS // P
KD = DIM // P
HIDDEN = 768
KH = HIDDEN // P
INNER = 4
OUTER = CHUNKS // INNER
LAST = OUTER - 1
STRIDES = (1, 2, 4)
FF_PARTS = 6
HI, LO = 0, 1
SCALE = 1.0 / 127.0
EPS = 1e-5
SPLIT = ((HI, HI), (HI, LO), (LO, HI))
H_SLOTS = 3


def build(nc, x, table, wu, bu, wg, bg, a_t, a_n, bm, b_n, cm, d, w_gate, w_up, w_down, out):
    ctx = ExitStack()
    phase1 = ExitStack()
    phase2 = ExitStack()
    with ctx:
        def sb(name, shape, dt, stack=ctx):
            return stack.enter_context(nc.sbuf_tensor(name, shape, dt))

        def sem(name):
            return ctx.enter_context(nc.semaphore(name))

        hres = sb("hres", [P, STEPS * GROUPS, DIM], F32)
        w_ff = sb("w_ff", [P, 2, FF_PARTS * HIDDEN], F32R)
        xn = sb("xn", [P, GROUPS, DIM], F32)
        xT = sb("xT", [P, 2, KD, COLS], F32R)
        sT = sb("sT", [P, 2, KD, COLS], F32R)
        mats = sb("mats", [P, 3, 2, KD, DIM], F32R)
        work = sb("work", [P, 4, COLS], F32)
        ident = sb("ident", [P, P], F32)
        bias = sb("bias", [P, 2, KD], F32)
        bn = sb("bn", [P, GROUPS, 6], F32)
        mv = sb("mv", [P, GROUPS, 2], F32)
        var_eps = sb("var_eps", [P, GROUPS], F32)
        rstd = sb("rstd", [P, GROUPS], F32)
        neg_half = sb("neg_half", [P, GROUPS], F32)
        lo_max = sb("lo_max", [P, FF_PARTS + 1], F32)
        lo_all = sb("lo_all", [P, 1], F32)
        wide = sb("wide", [P, 1], I32)
        m16 = sb("m16", [P, KD, DIM], F32)

        w_gu = w_ff[:, :, 0:4 * HIDDEN].rearrange("p s (k n) -> p s k n", k=KD)
        w_dn = w_ff[:, :, 4 * HIDDEN:].rearrange("p s (k n) -> p s k n", k=KH)
        a2t, ct, cat = (mats[:, n] for n in range(3))
        gelu, tanh = work[:, 0:2, :], work[:, 2:4, :]
        s_end = work[:, 0:2, :]
        start = work[:, 2:4, :]
        ends_i = s_end.rearrange("p k (bq i) -> p k i bq", i=INNER)
        sT_i = sT.rearrange("p s k (bq i) -> p s k i bq", i=INNER)
        start_i = start.rearrange("p k (bq i) -> p k i bq", i=INNER)
        start_q = start.rearrange("p k (b q i) -> p k i q b", q=OUTER, i=INNER)[:, :, 0]
        m64 = xn[:, 0:2, :]
        group_end = xn[:, 2, :].rearrange("p (k bq) -> p k bq", k=KD)
        group_end_q = xn[:, 2, :].rearrange("p (k b q) -> p k q b", k=KD, q=OUTER)
        silu = work[:, 0:2, :]
        hid = work[:, 2:4, :]

        w1 = sb("w1", [P, 5, 2, KD, DIM], F32R, phase1)
        v = sb("v", [P, KD, COLS], F32, phase1)
        vT = sb("vT", [P, 2, KD, COLS], F32R, phase1)
        bv = sb("bv", [P, KD, COLS], F32, phase1)
        raw = sb("raw", [P, 7, KD, DIM], F32, phase1)
        stage = sb("stage", [P, 2, GROUPS, DIM], F32, phase1)
        idx_t = sb("idx_t", [P, 2, GROUPS], I32, phase1)
        idx = sb("idx", [P, GROUPS, STEPS], I32, phase1)
        d_row = sb("d_row", [P, DIM], F32, phase1)
        wut, wgt, bt, abt, cbt = (w1[:, n] for n in range(5))
        early = hres[:, (STEPS - 3) * GROUPS:, :].rearrange("p (b s k) n -> p b s k n", b=3, s=2)
        powers_of_a = [(raw[:, 0], raw[:, 1]), (early[:, 0, 0], early[:, 0, 1]), (early[:, 1, 0], early[:, 1, 1]),
                       (early[:, 2, 0], early[:, 2, 1]), (m16[:, :, :], raw[:, 3]), (raw[:, 4], raw[:, 5]),
                       (m64, raw[:, 0]), (raw[:, 1], raw[:, 2]), (raw[:, 6], None)]
        m48 = raw[:, 3]
        raw_gu = hres[:, (STEPS - 3) * GROUPS:, :].rearrange("p b n -> p (b n)").rearrange(
            "p (a k n) -> p a k n", a=2, k=KD).bitcast(I32)
        raw_dn = raw[:, 0:3, :, :].rearrange("p a k n -> p (a k) n").bitcast(I32)
        phase1.close()
        s_in = sb("s_in", [P, KD, COLS], F32, phase2)
        pT = sb("pT", [P, 2, KD, COLS], F32R, phase2)
        hT = sb("hT", [P, H_SLOTS, 2, COLS], F32R, phase2)
        phase2.close()
        bv_dram = nc.dram_tensor("bv_dram", (PAIRS, P, KD, COLS), F32, kind="Internal").ap()

        xt_ps = ctx.enter_context(nc.psum_tensor("xt_ps", [P, 2, COLS], F32))
        up_ps = ctx.enter_context(nc.psum_tensor("up_ps", [P, 4, COLS], F32))
        st_ps = ctx.enter_context(nc.psum_tensor("st_ps", [P, 2, COLS], F32))
        tok_ps = xt_ps[:, :, :].rearrange("p b (g n) -> p b g n", n=DIM)
        dn_ps = st_ps[:, :, :].rearrange("p b (g n) -> p b g n", n=DIM)

        ld_idx, ld_a, ld_ug, ld_mix, ld_w, ld_small, ld_gu, ld_dn = (
            sem(n) for n in ("ld_idx", "ld_a", "ld_ug", "ld_mix", "ld_w", "ld_small", "ld_gu", "ld_dn"))
        bv_stored = sem("bv_stored")
        bv_loaded = sem("bv_loaded")
        gathered = [sem("gathered0"), sem("gathered1")]
        idx_set = sem("idx_set")
        const_set = sem("const_set")
        ident_set = sem("ident_set")
        rows_in = sem("rows_in")
        hres_set = sem("hres_set")
        bn_set = sem("bn_set")
        mv_set = sem("mv_set")
        eps_set = sem("eps_set")
        rstd_set = sem("rstd_set")
        xn_set = sem("xn_set")
        xt_done = sem("xt_done")
        xhi_set = sem("xhi_set")
        xlo_set = sem("xlo_set")
        whi_set = sem("whi_set")
        wlo_set = sem("wlo_set")
        ffhi_set = sem("ffhi_set")
        fflo_set = sem("fflo_set")
        lomax_set = sem("lomax_set")
        loall_set = sem("loall_set")
        wide_set = sem("wide_set")
        bias_set = sem("bias_set")
        pow_done = sem("pow_done")
        m48_done, m48_set = sem("m48_done"), sem("m48_set")
        pow_set = sem("pow_set")
        ug_done = sem("ug_done")
        act_set = sem("act_set")
        v_set = sem("v_set")
        vhi_set = sem("vhi_set")
        vlo_set = sem("vlo_set")
        mix_done = sem("mix_done")
        mixhi_set = sem("mixhi_set")
        mixlo_set = sem("mixlo_set")
        bv_done = sem("bv_done")
        s_done = sem("s_done")
        bvcopy_set = sem("bvcopy_set")
        send_set = sem("send_set")
        shi_set = sem("shi_set")
        slo_set = sem("slo_set")
        y_done = sem("y_done")
        y_added = sem("y_added")
        early_set = sem("early_set")
        zero_set = sem("zero_set")
        start_set = sem("start_set")
        bst_done = sem("bst_done")
        starthi_set = sem("starthi_set")
        startlo_set = sem("startlo_set")
        p_done = sem("p_done")
        p_set = sem("p_set")
        phi_set = sem("phi_set")
        plo_set = sem("plo_set")
        yt_done = sem("yt_done")
        yt_added = sem("yt_added")
        gu_done = sem("gu_done")
        silu_set = sem("silu_set")
        hid_set = sem("hid_set")
        hhi_set = sem("hhi_set")
        hlo_set = sem("hlo_set")
        dn_done = sem("dn_done")
        out_set = sem("out_set")
        stored = sem("stored")

        block = ctx.enter_context(nc.Block())
        out_v = out.rearrange("(g p j) d -> p g j d", p=P, j=STEPS)

        def inside(t, first, end):
            return first <= t < end if isinstance(t, int) else True

        carrier = {e.engine: e.alloc_register("wait_carrier") for e in (nc.vector, nc.gpsimd)}

        def wait_alone(eng, semaphore, count):
            if not isinstance(count, int):
                eng.reg_add(carrier[eng.engine], count, 0)
                count = carrier[eng.engine]
            eng.wait_ge(const_set, 2)
            eng.wait_ge(semaphore, count)

        def tiles(t):
            return hres[:, bass.ds(t * GROUPS, GROUPS), :]

        @block.sync
        def _(sp):
            sp.dma_start(idx[:, :, :], x.rearrange("(g p j) -> p g j", p=P, j=STEPS)).then_inc(ld_idx, 16)

            def load(n, w, loaded):
                sp.dma_start(raw[:, n, :, :], w.rearrange("(k p) n -> p k n", p=P)).then_inc(loaded, 16)

            load(0, a_t, ld_a)
            load(1, a_n, ld_a)
            load(2, wu, ld_ug)
            load(3, wg, ld_ug)
            load(6, b_n, ld_mix)
            load(5, cm, ld_mix)
            sp.dma_start(d_row[:, :], d.partition_broadcast(P)).then_inc(ld_small, 16)
            with nc.allow_non_contiguous_dma("two vectors of 256 values"):
                sp.dma_start(bias[:, 0, :], bu.rearrange("(k p) -> p k", p=P)).then_inc(ld_small, 16)
                sp.dma_start(bias[:, 1, :], bg.rearrange("(k p) -> p k", p=P)).then_inc(ld_small, 16)
            load(4, bm, ld_w)
            sp.wait_ge(pow_done, 7)
            sp.wait_ge(whi_set, 5)
            sp.wait_ge(wlo_set, 5)
            sp.dma_start(raw_gu[:, 0], w_gate.rearrange("(k p) n -> p k n", p=P)).then_inc(ld_gu, 16)
            sp.dma_start(raw_gu[:, 1], w_up.rearrange("(k p) n -> p k n", p=P)).then_inc(ld_gu, 16)
            sp.wait_ge(mix_done, 3)
            sp.dma_start(raw_dn, w_down.rearrange("(k p) n -> p k n", p=P)).then_inc(ld_dn, 16)
            with sp.Fori(0, PAIRS) as i:
                sp.wait_ge(bvcopy_set, 2 * i + 2)
                sp.dma_start(bv_dram[i], bv[:, :, :]).then_inc(bv_stored, 16)
            sp.wait_ge(bv_stored, 16 * PAIRS)

            def load_bv(i):
                sp.dma_start(s_in[:, :, :], bv_dram[i]).then_inc(bv_loaded, 16)

            def store(j):
                sp.wait_ge(out_set, 2 * j + 2)
                sp.dma_start(out_v[:, :, j, :], tiles(j)).then_inc(stored, 16)

            load_bv(0)
            sp.wait_ge(plo_set, 2)
            load_bv(1)
            with sp.Fori(0, PAIRS - 2) as i:
                store(2 * i)
                store(2 * i + 1)
                load_bv(i + 2)
            with sp.Fori(STEPS - 4, STEPS) as j:
                store(j)
            sp.wait_ge(stored, 16 * STEPS)

        @block.gpsimd
        def _(pool):
            pool.memset(ident[:, :], 0.0).then_inc(const_set, 1)
            pool.memset(neg_half[:, :], -0.5).then_inc(const_set, 1)
            pool.wait_ge(const_set, 2)
            pool.affine_select(out=ident[:, :], in_=ident[:, :], compare_op=ALU.not_equal, fill=1.0, base=0,
                               pattern=[[-1, P]], channel_multiplier=1).then_inc(ident_set, 1)
            pool.wait_ge(ld_idx, 16)

            def gather(j, p):
                pool.tensor_copy(idx_t[:, p, :], idx[:, :, j]).then_inc(idx_set, 1)
                wait_alone(pool, idx_set, j + 1)
                for g in range(GROUPS):
                    pool.indirect_dma_start(
                        out=stage[:, p, g, :], out_offset=None, in_=table,
                        in_offset=bass.IndirectOffsetOnAxis(ap=idx_t[:, p, g:g + 1], axis=0),
                    ).then_inc(gathered[p], 16)

            def rstd_of(n):
                wait_alone(pool, mv_set, n + 1)
                pool.tensor_scalar(var_eps[:, :], mv[:, :, 1], EPS, None, ALU.add).then_inc(eps_set, 1)
                pool.wait_ge(eps_set, n + 1)
                pool.tensor_tensor(rstd[:, :], var_eps[:, :], neg_half[:, :], ALU.pow).then_inc(rstd_set, 1)

            gather(0, 0)
            gather(1, 1)
            pool.wait_ge(ld_small, 48)

            def tile_in(j, p, n_before, more):
                pool.wait_ge(gathered[p], (n_before + 1) * GROUPS * 16)
                pool.sem_inc(rows_in, 1)
                rstd_of(j)
                pool.tensor_tensor(tiles(j), stage[:, p, :, :],
                                   d_row[:, None, :].to_broadcast([P, GROUPS, DIM]), ALU.add).then_inc(hres_set, 1)
                if more:
                    pool.wait_ge(xn_set, j + 1)
                    pool.wait_ge(hres_set, j + 1)
                    gather(j + 2, p)

            def tiles_in(i, more=True):
                tile_in(2 * i, 0, i, more)
                tile_in(2 * i + 1, 1, i, more)

            with pool.Fori(0, 6) as i:
                tiles_in(i)
            pool.wait_ge(fflo_set, 2)
            tiles_in(6)
            tiles_in(7, False)

            pool.wait_ge(lomax_set, FF_PARTS + 1)
            pool.partition_all_reduce(lo_all[:, :], lo_max[:, FF_PARTS:], P,
                                      bass.bass_isa.ReduceOp.max).then_inc(loall_set, 1)

            with pool.Fori(STEPS, 2 * STEPS) as n:
                rstd_of(n)

        @block.tensor
        def _(pe):
            def product(ps, w, m, r, first=True, last=True, **more):
                n = 0
                for k in range(KD):
                    for ws, rs in SPLIT:
                        mm = pe.matmul(ps, w[:, ws, k, m * P:(m + 1) * P], r[:, rs, k, :],
                                       start=first and n == 0, stop=last and n == KD * len(SPLIT) - 1, **more)
                        n += 1
                return mm

            def transposes(n):
                pe.wait_ge(xn_set, n + 1)
                for k in range(KD):
                    for g in range(GROUPS):
                        t = pe.transpose(xt_ps[:, k, g * P:(g + 1) * P], xn[:, g, k * P:(k + 1) * P], ident[:, :])
                    t.then_inc(xt_done, 1)

            def tokens(w, r, done, banks=tok_ps):
                for b in range(2):
                    for g in range(2):
                        n = 0
                        for k in range(KD):
                            for ws, rs in SPLIT:
                                c = (2 * b + g) * P
                                mm = pe.matmul(banks[:, b, g, :], w[:, ws, k, c:c + P], r[:, rs, k, :],
                                               start=n == 0, stop=n == KD * len(SPLIT) - 1)
                                n += 1
                    mm.then_inc(done, 1)

            def small(ps, w, moving):
                for m in range(KD):
                    for k in range(KD):
                        mm = pe.matmul(ps[:, m * DIM:(m + 1) * DIM], w[:, k, m * P:(m + 1) * P], moving[:, k, :],
                                       start=k == 0, stop=k == KD - 1)
                return mm

            def power(r, ps):
                if r == 0:
                    pe.wait_ge(ld_a, 32)
                else:
                    pe.wait_ge(pow_set, 2 * r)
                flipped, plain = powers_of_a[r]
                small(ps, plain, flipped).then_inc(pow_done, 1)

            def power_plain(r, ps):
                pe.wait_ge(pow_set, 2 * r + 1)
                flipped = powers_of_a[r + 1][0]
                for k in range(KD):
                    for m in range(KD):
                        t = pe.transpose(ps[:, k * DIM + m * P:k * DIM + (m + 1) * P],
                                         flipped[:, m, k * P:(k + 1) * P], ident[:, :])
                t.then_inc(pow_done, 1)

            def ug(j, m):
                pe.wait_ge(xlo_set, 2 * j + 2)
                if inside(j, 1, STEPS):
                    pe.wait_ge(act_set, 2 * j + m - 1)
                product(up_ps[:, 2 * m, :], wut, m, xT)
                product(up_ps[:, 2 * m + 1, :], wgt, m, xT).then_inc(ug_done, 1)

            def even_states(i):
                pe.wait_ge(vlo_set, 4 * i + 2)
                if inside(i, 1, PAIRS):
                    pe.wait_ge(slo_set, 2 * i)
                else:
                    pe.wait_ge(pow_set, 8)
                for m in range(KD):
                    product(st_ps[:, m, :], abt, m, vT, last=False)

            def odd_states(i):
                pe.wait_ge(vlo_set, 4 * i + 4)
                if not inside(i, 1, PAIRS):
                    pe.wait_ge(wlo_set, 5)
                for m in range(KD):
                    product(st_ps[:, m, :], bt, m, vT, first=False).then_inc(bv_done, 1)

            def carried_states(i):
                for m in range(KD):
                    pe.wait_ge(bvcopy_set, 2 * i + m + 1)
                    product(st_ps[:, m, :], a2t, m, sT, first=False, skip_group_check=True).then_inc(s_done, 1)

            def outputs(i):
                if inside(i, 0, PAIRS - 1):
                    pe.wait_ge(xlo_set, 4 * i + 6)
                tokens(vT, cbt, y_done)

            def even_step(i):
                ug(2 * i + 1, 0)
                if not inside(i, 1, PAIRS):
                    power_plain(3, st_ps[:, 1])
                if inside(i, 0, PAIRS - 1):
                    transposes(2 * i + 2)
                ug(2 * i + 1, 1)
                even_states(i)

            def odd_step(i):
                if inside(i, 0, PAIRS - 1):
                    ug(2 * i + 2, 0)
                outputs(i)
                if not inside(i, 0, PAIRS - 1):
                    power_plain(4, up_ps[:, 1])
                if inside(i, 0, PAIRS - 1):
                    ug(2 * i + 2, 1)
                else:
                    power(5, up_ps[:, 2])
                if inside(i, 1, PAIRS):
                    odd_states(i)
                if inside(i, 0, PAIRS - 1):
                    pe.wait_ge(y_added, 2 * i + 2)
                    transposes(2 * i + 3)
                else:
                    power_plain(5, up_ps[:, 3])
                if inside(i, 1, PAIRS):
                    carried_states(i)
                else:
                    odd_states(i)

            power(0, st_ps[:, 0])
            pe.wait_ge(ld_mix, 32)
            small(up_ps[:, 0, :], raw[:, 6], raw[:, 0]).then_inc(mix_done, 1)
            pe.wait_ge(ident_set, 1)
            power_plain(0, st_ps[:, 1])
            small(up_ps[:, 1, :], raw[:, 6], raw[:, 5]).then_inc(mix_done, 1)
            small(up_ps[:, 2, :], raw[:, 1], raw[:, 5]).then_inc(mix_done, 1)
            transposes(0)
            power(1, st_ps[:, 0])
            pe.wait_ge(wlo_set, 2)
            pe.wait_ge(mixlo_set, 3)
            ug(0, 0)
            power_plain(1, st_ps[:, 1])
            ug(0, 1)
            power(2, st_ps[:, 0])
            transposes(1)
            power_plain(2, st_ps[:, 1])
            power(3, st_ps[:, 0])
            even_step(0)
            odd_step(0)
            with pe.Fori(1, PAIRS - 1) as i:
                even_step(i)
                odd_step(i)
            even_step(PAIRS - 1)
            pe.wait_ge(act_set, 2 * STEPS)
            power(4, up_ps[:, 0])
            odd_step(PAIRS - 1)

            def boundary(bank, matrix, state, cols, count):
                pe.wait_ge(start_set, count)
                for m in range(KD):
                    for k in range(KD):
                        mm = pe.matmul(bank[:, m * cols:(m + 1) * cols], matrix[:, k, m * P:(m + 1) * P],
                                       state(k), start=k == 0, stop=k == KD - 1)
                mm.then_inc(bst_done, 1)

            def inner(i):
                boundary(st_ps[:, 0], m16, lambda k: start_i[:, k, i, :], BATCH * OUTER, i)

            def outer(n):
                stride = STRIDES[n]
                boundary(st_ps[:, 0], powers_of_a[6 + n][0], lambda k: group_end_q[:, k, 0:LAST - stride, :],
                         BATCH * (LAST - stride), INNER + n)

            small(up_ps[:, 2, :], powers_of_a[5][1], m16).then_inc(m48_done, 1)
            inner(1)
            power(6, up_ps[:, 0])
            inner(2)
            power_plain(6, up_ps[:, 1])
            inner(3)
            power(7, up_ps[:, 3])
            for n in range(len(STRIDES)):
                outer(n)
            pe.wait_ge(zero_set, 1)
            pe.wait_ge(early_set, 1)
            pe.wait_ge(m48_set, 1)
            for bank, matrix in ((xt_ps[:, 0], m16), (xt_ps[:, 1], powers_of_a[5][0]), (st_ps[:, 0], m48)):
                boundary(bank, matrix, lambda k: start_i[:, k, 0, :], BATCH * OUTER, INNER + len(STRIDES))

            def true_states(ps, state):
                for m in range(KD):
                    product(ps[:, m, :], a2t, m, state).then_inc(p_done, 1)

            def true_outputs(j, odd, banks=tok_ps):
                if odd:
                    pe.wait_ge(plo_set, j + 1)
                if isinstance(j, int) and j == 0:
                    tokens(sT, cat, yt_done)
                else:
                    tokens(pT, ct if odd else cat, yt_done, banks)

            def phase_2(lo_weights):
                parts = SPLIT if lo_weights else SPLIT[:2]

                def gate_up(j, m):
                    if m == 0:
                        pe.wait_ge(xlo_set, 2 * (j + STEPS) + 2)
                    if m >= 2 or inside(j, 1, STEPS):
                        pe.wait_ge(hid_set, KH * j + m - 1)
                    for side in range(2):
                        n = 0
                        for k in range(KD):
                            for ws, rs in parts:
                                c = side * HIDDEN + m * P
                                mm = pe.matmul(up_ps[:, 2 * (m % 2) + side, :], w_gu[:, ws, k, c:c + P],
                                               xT[:, rs, k, :], start=n == 0, stop=n == KD * len(parts) - 1)
                                n += 1
                    mm.then_inc(gu_done, 1)

                def down(j, m):
                    pe.wait_ge(hlo_set, KH * j + m + 1)
                    if m == 0:
                        if inside(j, 1, STEPS):
                            pe.wait_ge(out_set, 2 * j)
                        else:
                            pe.wait_ge(yt_added, 4)
                    for g in range(GROUPS):
                        for n, (ws, hs) in enumerate(parts):
                            mm = pe.matmul(dn_ps[:, g // 2, g % 2, :],
                                           hT[:, m % H_SLOTS, hs, g * P:(g + 1) * P], w_dn[:, ws, m, :],
                                           start=m == 0 and g % 2 == 0 and n == 0,
                                           stop=m == KH - 1 and n == len(parts) - 1, skip_group_check=True)
                    mm.then_inc(dn_done, 1)

                def step_2(j, odd):
                    gate_up(j, 0)
                    if inside(j, 1, STEPS - 1):
                        true_outputs(j + 1, not odd)
                    if inside(j, 1, STEPS):
                        down(j - 1, KH - 2)
                    gate_up(j, 1)
                    if inside(j, 1, STEPS):
                        down(j - 1, KH - 1)
                    gate_up(j, 2)
                    if odd and inside(j, 0, STEPS - 1):
                        pe.wait_ge(yt_added, 2 * j + 4)
                        true_states(xt_ps, pT)
                    gate_up(j, 3)
                    down(j, 0)
                    gate_up(j, 4)
                    if odd and inside(j, 0, STEPS - 1):
                        pe.wait_ge(p_set, j + 3)
                    if inside(j, 0, STEPS - 1):
                        transposes(STEPS + j + 1)
                    gate_up(j, 5)
                    down(j, 1)
                    down(j, 2)
                    down(j, 3)

                step_2(0, False)
                with pe.Fori(1, PAIRS) as i:
                    step_2(2 * i - 1, True)
                    step_2(2 * i, False)
                step_2(STEPS - 1, True)
                down(STEPS - 1, KH - 2)
                down(STEPS - 1, KH - 1)

            pe.wait_ge(startlo_set, INNER)
            pe.wait_ge(y_added, 2 * PAIRS)
            true_outputs(0, False)
            true_states(st_ps, sT)
            pe.wait_ge(yt_added, 2)
            transposes(STEPS)
            true_outputs(1, True, dn_ps)
            pe.wait_ge(wide_set, 1)
            pe.wait_ge(fflo_set, 3)
            is_wide = pe.value_load(wide[0:1, 0:1], min_val=0, max_val=1)
            with pe.If(is_wide == 0):
                phase_2(False)
            with pe.Else():
                phase_2(True)

        @block.scalar
        def _(act):
            def w_hi(dst, src):
                act.activation(dst[:, HI], src, ACT.Copy).then_inc(whi_set, 1)

            act.preload_act_table(ACT.Gelu)
            act.wait_ge(ld_ug, 32)
            w_hi(wut, raw[:, 2])
            w_hi(wgt, raw[:, 3])
            act.wait_ge(ld_mix, 32)
            w_hi(ct, raw[:, 5])
            act.wait_ge(ld_w, 16)
            w_hi(bt, raw[:, 4])
            act.wait_ge(pow_set, 1)
            w_hi(a2t, powers_of_a[1][0])
            for n, dst in enumerate((abt, cbt, cat)):
                act.wait_ge(mix_done, n + 1)
                act.activation(dst[:, HI], up_ps[:, n, :].rearrange("p (k n) -> p k n", k=KD),
                               ACT.Copy).then_inc(mixhi_set, 1)

            def x_hi(n):
                for k in range(KD):
                    act.wait_ge(xt_done, 2 * n + k + 1)
                    act.activation(xT[:, HI, k, :], xt_ps[:, k, :], ACT.Copy).then_inc(xhi_set, 1)

            def gates(j, m):
                act.wait_ge(ug_done, 2 * j + m + 1)
                if inside(j, 1, STEPS):
                    act.wait_ge(v_set, 2 * j + m - 1)
                act.activation(gelu[:, m, :], up_ps[:, 2 * m, :], ACT.Gelu, bias=bias[:, 0, m:m + 1])
                act.activation(tanh[:, m, :], up_ps[:, 2 * m + 1, :], ACT.Tanh, bias=bias[:, 1, m:m + 1],
                               scale=0.5).then_inc(act_set, 1)

            def v_hi(j, odd, i):
                if odd:
                    act.wait_ge(y_done, 2 * i + 2)
                elif inside(i, 1, PAIRS):
                    act.wait_ge(bv_done, 2 * i)
                for m in range(KD):
                    act.wait_ge(v_set, 2 * j + m + 1)
                    act.activation(vT[:, HI, m, :], v[:, m, :], ACT.Copy).then_inc(vhi_set, 1)

            def bv_copy(i):
                if inside(i, 1, PAIRS):
                    act.wait_ge(bv_stored, 16 * i)
                for m in range(KD):
                    act.wait_ge(bv_done, 2 * i + m + 1)
                    act.activation(bv[:, m, :], st_ps[:, m, :], ACT.Copy).then_inc(bvcopy_set, 1)

            def s_hi(i):
                if inside(i, 1, PAIRS):
                    act.wait_ge(s_done, 2 * i)
                for m in range(KD):
                    act.activation(sT[:, HI, m, :], st_ps[:, m, :], ACT.Copy).then_inc(shi_set, 1)

            def even_step(i):
                gates(2 * i + 1, 0)
                if inside(i, 0, PAIRS - 1):
                    act.wait_ge(ug_done, 4 * i + 4)
                    x_hi(2 * i + 2)
                gates(2 * i + 1, 1)

            def odd_step(i):
                if inside(i, 0, PAIRS - 1):
                    gates(2 * i + 2, 0)
                v_hi(2 * i + 1, True, i)
                if inside(i, 0, PAIRS - 1):
                    gates(2 * i + 2, 1)
                if inside(i, 1, PAIRS):
                    bv_copy(i)
                if inside(i, 0, PAIRS - 1):
                    x_hi(2 * i + 3)
                if not inside(i, 1, PAIRS):
                    bv_copy(i)
                if inside(i, 0, PAIRS - 1):
                    v_hi(2 * i + 2, False, i + 1)
                    s_hi(i)

            x_hi(0)
            act.wait_ge(bias_set, 1)
            gates(0, 0)
            gates(0, 1)
            x_hi(1)
            v_hi(0, False, 0)

            def ff_hi(dst, src, semaphore, count):
                act.wait_ge(semaphore, count)
                act.activation(dst, src, ACT.Copy).then_inc(ffhi_set, 1)

            even_step(0)
            odd_step(0)
            even_step(1)
            ff_hi(w_gu[:, HI, :, 0:HIDDEN], raw_gu[:, 0], ld_gu, 32)
            odd_step(1)
            even_step(2)
            ff_hi(w_gu[:, HI, :, HIDDEN:], raw_gu[:, 1], ld_gu, 32)
            odd_step(2)
            even_step(3)
            ff_hi(w_dn[:, HI, :, :], raw_dn, ld_dn, 16)
            odd_step(3)
            with act.Fori(4, PAIRS - 1) as i:
                even_step(i)
                odd_step(i)
            even_step(PAIRS - 1)
            odd_step(PAIRS - 1)
            act.wait_ge(s_done, 2 * PAIRS - 2)
            for m in range(KD):
                act.activation(s_end[:, m, :], st_ps[:, m, :], ACT.Copy).then_inc(send_set, 1)

            act.preload_act_table(ACT.Silu)
            act.wait_ge(zero_set, 1)
            act.wait_ge(early_set, 1)
            for i in range(INNER):
                act.wait_ge(start_set, INNER + len(STRIDES) + i)
                act.activation(sT_i[:, HI, :, i, :], start_i[:, :, i, :], ACT.Copy).then_inc(starthi_set, 1)

            def true_hi(i):
                if inside(i, 1, PAIRS):
                    act.wait_ge(yt_done, 4 * i + 2)
                act.wait_ge(p_done, 2 * i + 2)
                for m in range(KD):
                    act.wait_ge(p_set, 2 * i + m + 1)
                    act.activation(pT[:, HI, m, :], s_in[:, m, :], ACT.Copy).then_inc(phi_set, 1)

            def silu_of(j, m):
                act.wait_ge(gu_done, KH * j + m + 1)
                if m >= 2 or inside(j, 1, STEPS):
                    act.wait_ge(hid_set, KH * j + m - 1)
                act.activation(silu[:, m % 2, :], up_ps[:, 2 * (m % 2), :], ACT.Silu,
                               scale=SCALE).then_inc(silu_set, 1)

            def hid_hi(j, m):
                act.wait_ge(hid_set, KH * j + m + 1)
                if m >= H_SLOTS or inside(j, 1, STEPS):
                    act.wait_ge(dn_done, KH * j + m + 1 - H_SLOTS)
                act.activation(hT[:, m % H_SLOTS, HI, :], hid[:, m % 2, :], ACT.Copy).then_inc(hhi_set, 1)

            def step_2(j, odd, i=None):
                for m in range(KH - 1):
                    silu_of(j, m)
                    if m > 0:
                        hid_hi(j, m - 1)
                    if m == 3 and odd and inside(j, 0, STEPS - 1):
                        true_hi(i)
                if inside(j, 0, STEPS - 1):
                    act.wait_ge(gu_done, KH * (j + 1))
                    x_hi(STEPS + j + 1)
                silu_of(j, KH - 1)
                hid_hi(j, KH - 2)
                hid_hi(j, KH - 1)

            true_hi(0)
            x_hi(STEPS)
            step_2(0, False)
            with act.Fori(1, PAIRS) as i:
                step_2(2 * i - 1, True, i)
                step_2(2 * i, False)
            step_2(STEPS - 1, True)

        @block.vector
        def _(dve):
            def w_lo(n, dst, src):
                dve.wait_ge(whi_set, n)
                dve.tensor_tensor(dst[:, LO], src, dst[:, HI].bitcast(F32), ALU.subtract).then_inc(wlo_set, 1)

            def mix_lo(n, dst):
                dve.wait_ge(mixhi_set, n + 1)
                dve.tensor_tensor(dst[:, LO], up_ps[:, n, :].rearrange("p (k n) -> p k n", k=KD),
                                  dst[:, HI].bitcast(F32), ALU.subtract).then_inc(mixlo_set, 1)

            def mean_variance(n):
                wait_alone(dve, bn_set, n + 1)
                for g in range(GROUPS):
                    last = dve.bn_aggr(mv[:, g, :], bn[:, g, :])
                last.then_inc(mv_set, 1)

            def norm_stats(n):
                if isinstance(n, int) and n < 2:
                    dve.wait_ge(gathered[n], GROUPS * 16)
                else:
                    wait_alone(dve, rows_in, n + 1)
                for g in range(GROUPS):
                    last = dve.bn_stats(bn[:, g, :], stage[:, n % 2, g, :])
                last.then_inc(bn_set, 1)
                mean_variance(n)

            def norm_apply(n, src):
                dve.wait_ge(rstd_set, n + 1)
                if not (isinstance(n, int) and n == 0):
                    dve.wait_ge(xt_done, 2 * n)
                for g in range(GROUPS):
                    rows = stage[:, n % 2, g, :] if src is stage else hres[:, (n - STEPS) * GROUPS + g, :]
                    last = dve.tensor_scalar(xn[:, g, :], rows, mv[:, g, 0:1], rstd[:, g:g + 1],
                                             ALU.subtract, ALU.mult)
                last.then_inc(xn_set, 1)

            def x_lo(n):
                for k in range(KD):
                    dve.wait_ge(xhi_set, 2 * n + k + 1)
                    dve.tensor_tensor(xT[:, LO, k, :], xt_ps[:, k, :], xT[:, HI, k, :].bitcast(F32),
                                      ALU.subtract).then_inc(xlo_set, 1)

            def gate(j, m):
                dve.wait_ge(act_set, 2 * j + m + 1)
                if inside(j, 1, STEPS):
                    dve.wait_ge(vlo_set, 2 * j + m - 1)
                dve.scalar_tensor_tensor(out=v[:, m, :], in0=tanh[:, m, :], scalar=1.0, in1=gelu[:, m, :],
                                         op0=ALU.add, op1=ALU.mult).then_inc(v_set, 1)

            def v_lo(j):
                for m in range(KD):
                    dve.wait_ge(vhi_set, 2 * j + m + 1)
                    dve.tensor_tensor(vT[:, LO, m, :], v[:, m, :], vT[:, HI, m, :].bitcast(F32),
                                      ALU.subtract).then_inc(vlo_set, 1)

            def s_lo(i):
                for m in range(KD):
                    dve.wait_ge(shi_set, 2 * i + m + 1)
                    dve.tensor_tensor(sT[:, LO, m, :], st_ps[:, m, :], sT[:, HI, m, :].bitcast(F32),
                                      ALU.subtract).then_inc(slo_set, 1)

            def add_half(j, t, b, done, added, banks=tok_ps):
                dve.wait_ge(done, 2 * t + b + 1)
                half = hres[:, bass.ds(j * GROUPS + 2 * b, 2), :]
                dve.scalar_tensor_tensor(out=half, in0=banks[:, b, :, :], scalar=0.5, in1=half,
                                         op0=ALU.mult, op1=ALU.add).then_inc(added, 1)

            def even_step(i):
                if not inside(i, 1, PAIRS):
                    power_out(3, 1, st_ps[:, 1])
                gate(2 * i + 1, 0)
                if inside(i, 0, PAIRS - 1):
                    x_lo(2 * i + 2)
                gate(2 * i + 1, 1)
                if inside(i, 0, PAIRS - 1):
                    norm_stats(2 * i + 3)
                    norm_apply(2 * i + 3, stage)

            def odd_step(i):
                if not inside(i, 0, PAIRS - 1):
                    power_out(4, 1, up_ps[:, 1])
                v_lo(2 * i + 1)
                for b in range(2):
                    add_half(2 * i, i, b, y_done, y_added)
                if inside(i, 0, PAIRS - 1):
                    gate(2 * i + 2, 0)
                    gate(2 * i + 2, 1)
                    if inside(i, 0, PAIRS - 2):
                        norm_stats(2 * i + 4)
                    x_lo(2 * i + 3)
                    v_lo(2 * i + 2)
                    if inside(i, 0, PAIRS - 2):
                        norm_apply(2 * i + 4, stage)
                    s_lo(i)

            def ff_lo(n, dst, src):
                dve.wait_ge(ffhi_set, n + 1)
                dve.tensor_tensor(dst[:, LO], src, dst[:, HI].bitcast(F32), ALU.subtract).then_inc(fflo_set, 1)

            def largest_lo(first):
                dve.wait_ge(fflo_set, 3)
                with dve.Fori(first, first + FF_PARTS // 2) as n:
                    dve.tensor_reduce(lo_max[:, bass.ds(n, 1)], w_ff[:, LO, bass.ds(n * HIDDEN, HIDDEN)].bitcast(F32),
                                      mybir.AxisListType.X, ALU.max, apply_absolute_value=True).then_inc(lomax_set, 1)

            def power_out(r, side, ps):
                dve.wait_ge(pow_done, 2 * r + side + 1)
                dve.tensor_copy(powers_of_a[r + 1][side], ps.rearrange("p (k n) -> p k n", k=KD)).then_inc(pow_set, 1)

            w_lo(1, wut, raw[:, 2])
            w_lo(2, wgt, raw[:, 3])
            power_out(0, 0, st_ps[:, 0])
            w_lo(3, ct, raw[:, 5])
            norm_stats(0)
            w_lo(4, bt, raw[:, 4])
            power_out(0, 1, st_ps[:, 1])
            mix_lo(0, abt)
            norm_apply(0, stage)
            mix_lo(1, cbt)
            mix_lo(2, cat)
            dve.wait_ge(ld_small, 48)
            dve.tensor_scalar(bias[:, 1, :], bias[:, 1, :], 0.5, None, ALU.mult).then_inc(bias_set, 1)
            x_lo(0)
            power_out(1, 0, st_ps[:, 0])
            norm_stats(1)
            w_lo(5, a2t, powers_of_a[1][0])
            power_out(1, 1, st_ps[:, 1])
            norm_apply(1, stage)
            gate(0, 0)
            power_out(2, 0, st_ps[:, 0])
            norm_stats(2)
            power_out(2, 1, st_ps[:, 1])
            gate(0, 1)
            x_lo(1)
            v_lo(0)
            norm_apply(2, stage)
            power_out(3, 0, st_ps[:, 0])
            even_step(0)
            odd_step(0)
            even_step(1)
            odd_step(1)
            ff_lo(0, w_gu[:, :, :, 0:HIDDEN], raw_gu[:, 0])
            even_step(2)
            odd_step(2)
            ff_lo(1, w_gu[:, :, :, HIDDEN:], raw_gu[:, 1])
            even_step(3)
            odd_step(3)
            ff_lo(2, w_dn, raw_dn)
            with dve.Fori(4, 6) as i:
                even_step(i)
                odd_step(i)
            largest_lo(0)
            even_step(6)
            odd_step(6)
            largest_lo(FF_PARTS // 2)
            even_step(7)
            power_out(4, 0, up_ps[:, 0])
            odd_step(7)
            power_out(5, 0, up_ps[:, 2])
            power_out(5, 1, up_ps[:, 3])

            dve.memset(start_q[:, :, 0, :], 0.0).then_inc(zero_set, 1)
            dve.wait_ge(send_set, 2)
            dve.tensor_copy(start_i[:, :, 1, :], ends_i[:, :, 0, :]).then_inc(start_set, 1)
            dve.wait_ge(m48_done, 1)
            dve.tensor_copy(m48, up_ps[:, 2, :].rearrange("p (k n) -> p k n", k=KD)).then_inc(m48_set, 1)

            def boundary(dst, bank, own, count):
                dve.wait_ge(bst_done, count)
                dve.tensor_tensor(dst, bank[:, 0:KD * BATCH * OUTER].rearrange("p (k c) -> p k c", k=KD), own,
                                  ALU.add).then_inc(start_set, 1)

            boundary(start_i[:, :, 2, :], st_ps[:, 0], ends_i[:, :, 1, :], 1)
            power_out(6, 0, up_ps[:, 0])
            boundary(start_i[:, :, 3, :], st_ps[:, 0], ends_i[:, :, 2, :], 2)
            power_out(6, 1, up_ps[:, 1])
            boundary(group_end, st_ps[:, 0], ends_i[:, :, INNER - 1, :], INNER - 1)
            power_out(7, 0, up_ps[:, 3])
            for n, stride in enumerate(STRIDES):
                cols = BATCH * (LAST - stride)
                last = n == len(STRIDES) - 1
                if last:
                    dve.wait_ge(start_set, INNER + n)
                    dve.tensor_copy(start_q[:, :, 1:stride + 1, :],
                                    group_end_q[:, :, 0:stride, :]).then_inc(early_set, 1)
                dve.wait_ge(bst_done, INNER + n)
                dve.tensor_tensor(start_q[:, :, stride + 1:, :] if last else group_end_q[:, :, stride:LAST, :],
                                  st_ps[:, 0, 0:KD * cols].rearrange("p (k q b) -> p k q b", k=KD, b=BATCH),
                                  group_end_q[:, :, stride:LAST, :], ALU.add).then_inc(start_set, 1)

            def start_lo(i):
                dve.wait_ge(starthi_set, i + 1)
                dve.tensor_tensor(sT_i[:, LO, :, i, :], start_i[:, :, i, :], sT_i[:, HI, :, i, :].bitcast(F32),
                                  ALU.subtract).then_inc(startlo_set, 1)

            for n, bank in enumerate((xt_ps[:, 0], xt_ps[:, 1], st_ps[:, 0])):
                boundary(start_i[:, :, n + 1, :], bank, start_i[:, :, n + 1, :], INNER + len(STRIDES) + n)
                start_lo(n)
            start_lo(INNER - 1)
            dve.wait_ge(lomax_set, FF_PARTS)
            dve.tensor_reduce(lo_max[:, FF_PARTS:], lo_max[:, 0:FF_PARTS], mybir.AxisListType.X,
                              ALU.max).then_inc(lomax_set, 1)

            def true_sum(i, ps=xt_ps):
                dve.wait_ge(bv_loaded, 16 * i + 16)
                for m in range(KD):
                    dve.wait_ge(p_done, 2 * i + m + 1)
                    dve.tensor_tensor(s_in[:, m, :], ps[:, m, :], s_in[:, m, :], ALU.add).then_inc(p_set, 1)

            def true_lo(i):
                for m in range(KD):
                    dve.wait_ge(phi_set, 2 * i + m + 1)
                    dve.tensor_tensor(pT[:, LO, m, :], s_in[:, m, :], pT[:, HI, m, :].bitcast(F32),
                                      ALU.subtract).then_inc(plo_set, 1)

            def hid_lo(j, m):
                dve.wait_ge(hhi_set, KH * j + m + 1)
                dve.tensor_tensor(hT[:, m % H_SLOTS, LO, :], hid[:, m % 2, :],
                                  hT[:, m % H_SLOTS, HI, :].bitcast(F32), ALU.subtract).then_inc(hlo_set, 1)

            def hid_mul(j, m):
                dve.wait_ge(silu_set, KH * j + m + 1)
                if m >= 2 or inside(j, 1, STEPS):
                    dve.wait_ge(hlo_set, KH * j + m - 1)
                dve.tensor_tensor(hid[:, m % 2, :], up_ps[:, 2 * (m % 2) + 1, :], silu[:, m % 2, :],
                                  ALU.mult).then_inc(hid_set, 1)

            def add_down(j):
                dve.wait_ge(dn_done, KH * (j + 1))
                for b in range(2):
                    half = hres[:, bass.ds(j * GROUPS + 2 * b, 2), :]
                    dve.scalar_tensor_tensor(out=half, in0=dn_ps[:, b, :, :], scalar=SCALE * SCALE, in1=half,
                                             op0=ALU.mult, op1=ALU.add).then_inc(out_set, 1)

            def second_norm_stats(j):
                for b in range(2):
                    add_half(j, j, b, yt_done, yt_added, dn_ps if isinstance(j, int) and j == 1 else tok_ps)
                    wait_alone(dve, yt_added, 2 * j + b + 1)
                    for g in (2 * b, 2 * b + 1):
                        last = dve.bn_stats(bn[:, g, :], hres[:, j * GROUPS + g, :])
                last.then_inc(bn_set, 1)
                mean_variance(STEPS + j)

            def step_2(j, odd, i=None):
                hid_mul(j, 0)
                if inside(j, 1, STEPS - 1):
                    second_norm_stats(j + 1)
                for m in range(1, KH - 1):
                    hid_mul(j, m)
                    hid_lo(j, m - 1)
                    if m == 1 and inside(j, 1, STEPS):
                        add_down(j - 1)
                    if m == 2 and inside(j, 0, STEPS - 1):
                        if odd:
                            true_sum(i)
                        norm_apply(STEPS + j + 1, hres)
                if inside(j, 0, STEPS - 1):
                    if odd:
                        true_lo(i)
                    x_lo(STEPS + j + 1)
                hid_mul(j, KH - 1)
                hid_lo(j, KH - 2)
                hid_lo(j, KH - 1)

            second_norm_stats(0)
            true_sum(0, st_ps)
            norm_apply(STEPS, hres)
            true_lo(0)
            dve.wait_ge(loall_set, 1)
            dve.tensor_scalar(wide[:, :], lo_all[:, :], 0.0, None, ALU.is_gt).then_inc(wide_set, 1)
            x_lo(STEPS)
            second_norm_stats(1)
            step_2(0, False)
            with dve.Fori(1, PAIRS) as i:
                step_2(2 * i - 1, True, i)
                step_2(2 * i, False)
            step_2(STEPS - 1, True)
            add_down(STEPS - 1)


def kernel(**inputs):
    import numpy as np
    import concourse.bacc as bacc
    from concourse.bass_utils import run_bass_kernel_spmd

    get = {k: np.asarray(val) for k, val in inputs.items()}
    arrays = {
        "x": get["x"].reshape(-1),
        "table": get["L0_tok_W"].T,
        "wu": get["L0_attn_W_u"].T, "bu": get["L0_attn_b_u"],
        "wg": get["L0_attn_W_g"].T, "bg": get["L0_attn_b_g"],
        "a_t": get["L0_attn_A"].T, "a_n": get["L0_attn_A"],
        "bm": get["L0_attn_Bm"].T, "b_n": get["L0_attn_Bm"], "cm": get["L0_attn_Cm"].T, "d": get["L0_attn_D"],
        "w_gate": get["L0_ffn_w_gate"].T, "w_up": get["L0_ffn_w_up"].T, "w_down": get["L0_ffn_w_down"].T,
    }
    arrays = {k: np.ascontiguousarray(val) for k, val in arrays.items()}
    nc = bacc.Bacc("TRN2", target_bir_lowering=False, num_devices=1)
    args = [nc.dram_tensor(k, val.shape, mybir.dt.from_np(val.dtype), kind="ExternalInput").ap()
            for k, val in arrays.items()]
    out = nc.dram_tensor("out", (BATCH * SEQ, DIM), F32, kind="ExternalOutput").ap()
    build(nc, *args, out)
    r = run_bass_kernel_spmd(nc, [arrays], core_ids=[0])
    return r.results[0]["out"].reshape(BATCH, SEQ, DIM)
```
